# Optimizing a Trainium2 kernel written in Bass

```python
import numpy as np
import jax
import jax.numpy as jnp

def _softmax(x, axis=-1):
    return jax.nn.softmax(x, axis=axis)

def _gelu(x):
    return jax.nn.gelu(x, approximate=True)

def _silu(x):
    return jax.nn.silu(x)

def _sigmoid(x):
    return jax.nn.sigmoid(x)

def _layernorm(x, axis=-1, eps=1e-05):
    m = jnp.mean(x, axis=axis, keepdims=True)
    v = jnp.var(x, axis=axis, keepdims=True)
    return (x - m) / jnp.sqrt(v + eps)

def _scatter_add(tgt, idx, src, axis=0):
    return tgt.at[idx].add(src)

def _segment_sum(src, seg, n):
    return jax.ops.segment_sum(src, seg, n)
kernel_name = 'mk_sandwich_d1_jaxref_r8_98fb61'

def setup_inputs(seed: int=0):
    np.random.seed(seed)
    _w = jnp.asarray

    def _L0_attn_setup():
        import jax, jax.numpy as jnp
        import numpy as np

        def log_g(x):
            return jnp.where(x >= 0.0, jnp.log(jax.nn.relu(x) + 0.5), -jax.nn.softplus(-x))

        def _reference_tuple_inner(x, W_hg, W_out):
            H = W_hg.shape[0] // 2
            hg = jnp.einsum('btd,hd->bth', x, W_hg)
            hidden, gate = (hg[..., :H], hg[..., H:])
            log_coeffs = -jax.nn.softplus(gate)
            log_values = -jax.nn.softplus(-gate) + log_g(hidden)

            def combine(p1, p2):
                logA1, logB1 = p1
                logA2, logB2 = p2
                return (logA2 + logA1, jnp.logaddexp(logA2 + logB1, logB2))
            logA, logB = jax.lax.associative_scan(combine, (log_coeffs, log_values), axis=1)
            h = jnp.exp(logB)
            h_n = h[:, -1:]
            out = jnp.einsum('bth,oh->bto', h, W_out)
            return (out, h_n)
        key = jax.random.key(seed)
        k_x, k_w1, k_w2 = jax.random.split(key, 3)
        B, T, D_in, H, D_out = (4, 512, 128, 128, 128)
        x = jax.random.normal(k_x, (B, T, D_in), dtype=jnp.float32)
        W_hg = jax.random.normal(k_w1, (2 * H, D_in), dtype=jnp.float32) / np.sqrt(D_in)
        W_out = jax.random.normal(k_w2, (D_out, H), dtype=jnp.float32) / np.sqrt(H)
        return {'x': x, 'W_hg': W_hg, 'W_out': W_out}
    _L0_attn_in = _L0_attn_setup()

    def _L0_ffn_setup():
        import jax, jax.numpy as jnp
        import numpy as np
        DIM = 128
        DEPTH = 2
        HEADS = 8
        DIM_HEAD = 64
        WINDOW = 64
        INNER = HEADS * DIM_HEAD
        HID = int(DIM * 4 * 2 / 3)
        B, N = (2, 1024)
        QK_SCALE = 8.0

        def shift_token(t):
            t1, t2 = jnp.split(t, 2, axis=-1)
            t2 = jnp.pad(t2, ((0, 0), (1, 0), (0, 0)))[:, :-1]
            return jnp.concatenate([t1, t2], axis=-1)

        def l2norm(t):
            return t / jnp.clip(jnp.linalg.norm(t, axis=-1, keepdims=True), 1e-12)

        def rotate_half(x):
            x1, x2 = jnp.split(x, 2, axis=-1)
            return jnp.concatenate([-x2, x1], axis=-1)

        def rotary_xpos(q, k):
            n = q.shape[-2]
            half_idx = jnp.arange(0, DIM_HEAD, 2, dtype=jnp.float32)
            inv_freq = 1.0 / 10000.0 ** (half_idx / DIM_HEAD)
            t = jnp.arange(n, dtype=jnp.float32)
            freqs = t[:, None] * inv_freq[None, :]
            freqs = jnp.concatenate([freqs, freqs], axis=-1)
            base = (half_idx + 0.4 * DIM_HEAD) / (1.4 * DIM_HEAD)
            power = (t - n // 2) / float(WINDOW // 2)
            scale = base[None, :] ** power[:, None]
            scale = jnp.concatenate([scale, scale], axis=-1)
            cos, sin = (jnp.cos(freqs), jnp.sin(freqs))
            q = q * cos * scale + rotate_half(q) * sin * scale
            k = k * cos / scale + rotate_half(k) * sin / scale
            return (q, k)

        def local_attention(q, k, v):
            b, h, n, d = q.shape
            w = n // WINDOW
            bq = q.reshape(b, h, w, WINDOW, d) * QK_SCALE
            bk = k.reshape(b, h, w, WINDOW, d)
            bv = v.reshape(b, h, w, WINDOW, d)

            def look_around(t):
                p = jnp.pad(t, ((0, 0), (0, 0), (1, 0), (0, 0), (0, 0)))
                return jnp.concatenate([p[:, :, :w], p[:, :, 1:]], axis=3)
            bk, bv = (look_around(bk), look_around(bv))
            bt = jnp.arange(n).reshape(w, WINDOW)
            btp = jnp.pad(bt, ((1, 0), (0, 0)), constant_values=-1)
            btk = jnp.concatenate([btp[:w], btp[1:]], axis=1)
            sim = jnp.einsum('bhwid,bhwjd->bhwij', bq, bk)
            i = bt[:, :, None]
            j = btk[:, None, :]
            mask = (i < j) | (i > j + WINDOW) | (j == -1)
            sim = jnp.where(mask, -jnp.finfo(sim.dtype).max, sim)
            attn = jax.nn.softmax(sim, axis=-1)
            out = jnp.einsum('bhwij,bhwjd->bhwid', attn, bv)
            return out.reshape(b, h, n, d)

        def _layer(x, wqkv, qs, ksc, wo, lg, lb, w1, b1, w2, b2):
            b, n, _ = x.shape
            h = shift_token(x)
            qkv = h @ wqkv
            q, k, v = jnp.split(qkv, 3, axis=-1)
            to_heads = lambda t: t.reshape(b, n, HEADS, DIM_HEAD).transpose(0, 2, 1, 3)
            q, k, v = (to_heads(q), to_heads(k), to_heads(v))
            q = l2norm(q) * qs
            k = l2norm(k) * ksc
            q, k = rotary_xpos(q, k)
            o = local_attention(q, k, v)
            o = o.transpose(0, 2, 1, 3).reshape(b, n, INNER)
            x = x + o @ wo
            h = shift_token(x)
            mu = h.mean(-1, keepdims=True)
            var = h.var(-1, keepdims=True)
            h = (h - mu) / jnp.sqrt(var + 1e-05) * lg + lb
            h = h @ w1 + b1
            a, g = jnp.split(h, 2, axis=-1)
            h = a * jax.nn.gelu(g, approximate=False)
            x = x + h @ w2 + b2
            return x
        key = jax.random.key(seed)
        ks = jax.random.split(key, 6)
        return {'x': jax.random.normal(ks[0], (B, N, DIM), jnp.float32), 'wqkv': jax.random.normal(ks[1], (DEPTH, DIM, 3 * INNER), jnp.float32) * 0.02, 'q_scale': jnp.ones((DEPTH, DIM_HEAD), jnp.float32), 'k_scale': jnp.ones((DEPTH, DIM_HEAD), jnp.float32), 'wo': jax.random.normal(ks[2], (DEPTH, INNER, DIM), jnp.float32) * 0.02, 'ln_g': jnp.ones((DEPTH, DIM), jnp.float32), 'ln_b': jnp.zeros((DEPTH, DIM), jnp.float32), 'w1': jax.random.normal(ks[3], (DEPTH, DIM, 2 * HID), jnp.float32) * 0.02, 'b1': jnp.zeros((DEPTH, 2 * HID), jnp.float32), 'w2': jax.random.normal(ks[4], (DEPTH, HID, DIM), jnp.float32) * 0.02, 'b2': jnp.zeros((DEPTH, DIM), jnp.float32)}
    _L0_ffn_in = _L0_ffn_setup()
    _d = {'L0_attn_x': _L0_attn_in['x'], 'L0_attn_W_hg': _L0_attn_in['W_hg'], 'L0_attn_W_out': _L0_attn_in['W_out'], 'L0_ffn_wqkv': _L0_ffn_in['wqkv'], 'L0_ffn_q_scale': _L0_ffn_in['q_scale'], 'L0_ffn_k_scale': _L0_ffn_in['k_scale'], 'L0_ffn_wo': _L0_ffn_in['wo'], 'L0_ffn_ln_g': _L0_ffn_in['ln_g'], 'L0_ffn_ln_b': _L0_ffn_in['ln_b'], 'L0_ffn_w1': _L0_ffn_in['w1'], 'L0_ffn_b1': _L0_ffn_in['b1'], 'L0_ffn_w2': _L0_ffn_in['w2'], 'L0_ffn_b2': _L0_ffn_in['b2']}
    _x0 = _d['L0_attn_x']
    _d['L0_attn_x'] = jax.random.normal(jax.random.fold_in(jax.random.key(seed), 1), (1, 2048, 128), dtype=_x0.dtype)
    del _x0
    return _d

def reference(L0_attn_x, L0_attn_W_hg, L0_attn_W_out, L0_ffn_wqkv, L0_ffn_q_scale, L0_ffn_k_scale, L0_ffn_wo, L0_ffn_ln_g, L0_ffn_ln_b, L0_ffn_w1, L0_ffn_b1, L0_ffn_w2, L0_ffn_b2):

    def _L0_attn_ref(x, W_hg, W_out):
        import jax, jax.numpy as jnp
        import numpy as np

        def log_g(x):
            return jnp.where(x >= 0.0, jnp.log(jax.nn.relu(x) + 0.5), -jax.nn.softplus(-x))

        def _reference_tuple_inner(x, W_hg, W_out):
            H = W_hg.shape[0] // 2
            hg = jnp.einsum('btd,hd->bth', x, W_hg)
            hidden, gate = (hg[..., :H], hg[..., H:])
            log_coeffs = -jax.nn.softplus(gate)
            log_values = -jax.nn.softplus(-gate) + log_g(hidden)

            def combine(p1, p2):
                logA1, logB1 = p1
                logA2, logB2 = p2
                return (logA2 + logA1, jnp.logaddexp(logA2 + logB1, logB2))
            logA, logB = jax.lax.associative_scan(combine, (log_coeffs, log_values), axis=1)
            h = jnp.exp(logB)
            h_n = h[:, -1:]
            out = jnp.einsum('bth,oh->bto', h, W_out)
            return (out, h_n)
        return _reference_tuple_inner(x, W_hg, W_out)[0]

    def _L0_ffn_ref(x, wqkv, q_scale, k_scale, wo, ln_g, ln_b, w1, b1, w2, b2):
        import jax, jax.numpy as jnp
        import numpy as np
        DIM = 128
        DEPTH = 2
        HEADS = 8
        DIM_HEAD = 64
        WINDOW = 64
        INNER = HEADS * DIM_HEAD
        HID = int(DIM * 4 * 2 / 3)
        B, N = (2, 1024)
        QK_SCALE = 8.0

        def shift_token(t):
            t1, t2 = jnp.split(t, 2, axis=-1)
            t2 = jnp.pad(t2, ((0, 0), (1, 0), (0, 0)))[:, :-1]
            return jnp.concatenate([t1, t2], axis=-1)

        def l2norm(t):
            return t / jnp.clip(jnp.linalg.norm(t, axis=-1, keepdims=True), 1e-12)

        def rotate_half(x):
            x1, x2 = jnp.split(x, 2, axis=-1)
            return jnp.concatenate([-x2, x1], axis=-1)

        def rotary_xpos(q, k):
            n = q.shape[-2]
            half_idx = jnp.arange(0, DIM_HEAD, 2, dtype=jnp.float32)
            inv_freq = 1.0 / 10000.0 ** (half_idx / DIM_HEAD)
            t = jnp.arange(n, dtype=jnp.float32)
            freqs = t[:, None] * inv_freq[None, :]
            freqs = jnp.concatenate([freqs, freqs], axis=-1)
            base = (half_idx + 0.4 * DIM_HEAD) / (1.4 * DIM_HEAD)
            power = (t - n // 2) / float(WINDOW // 2)
            scale = base[None, :] ** power[:, None]
            scale = jnp.concatenate([scale, scale], axis=-1)
            cos, sin = (jnp.cos(freqs), jnp.sin(freqs))
            q = q * cos * scale + rotate_half(q) * sin * scale
            k = k * cos / scale + rotate_half(k) * sin / scale
            return (q, k)

        def local_attention(q, k, v):
            b, h, n, d = q.shape
            w = n // WINDOW
            bq = q.reshape(b, h, w, WINDOW, d) * QK_SCALE
            bk = k.reshape(b, h, w, WINDOW, d)
            bv = v.reshape(b, h, w, WINDOW, d)

            def look_around(t):
                p = jnp.pad(t, ((0, 0), (0, 0), (1, 0), (0, 0), (0, 0)))
                return jnp.concatenate([p[:, :, :w], p[:, :, 1:]], axis=3)
            bk, bv = (look_around(bk), look_around(bv))
            bt = jnp.arange(n).reshape(w, WINDOW)
            btp = jnp.pad(bt, ((1, 0), (0, 0)), constant_values=-1)
            btk = jnp.concatenate([btp[:w], btp[1:]], axis=1)
            sim = jnp.einsum('bhwid,bhwjd->bhwij', bq, bk)
            i = bt[:, :, None]
            j = btk[:, None, :]
            mask = (i < j) | (i > j + WINDOW) | (j == -1)
            sim = jnp.where(mask, -jnp.finfo(sim.dtype).max, sim)
            attn = jax.nn.softmax(sim, axis=-1)
            out = jnp.einsum('bhwij,bhwjd->bhwid', attn, bv)
            return out.reshape(b, h, n, d)

        def _layer(x, wqkv, qs, ksc, wo, lg, lb, w1, b1, w2, b2):
            b, n, _ = x.shape
            h = shift_token(x)
            qkv = h @ wqkv
            q, k, v = jnp.split(qkv, 3, axis=-1)
            to_heads = lambda t: t.reshape(b, n, HEADS, DIM_HEAD).transpose(0, 2, 1, 3)
            q, k, v = (to_heads(q), to_heads(k), to_heads(v))
            q = l2norm(q) * qs
            k = l2norm(k) * ksc
            q, k = rotary_xpos(q, k)
            o = local_attention(q, k, v)
            o = o.transpose(0, 2, 1, 3).reshape(b, n, INNER)
            x = x + o @ wo
            h = shift_token(x)
            mu = h.mean(-1, keepdims=True)
            var = h.var(-1, keepdims=True)
            h = (h - mu) / jnp.sqrt(var + 1e-05) * lg + lb
            h = h @ w1 + b1
            a, g = jnp.split(h, 2, axis=-1)
            h = a * jax.nn.gelu(g, approximate=False)
            x = x + h @ w2 + b2
            return x
        for l in range(DEPTH):
            x = _layer(x, wqkv[l], q_scale[l], k_scale[l], wo[l], ln_g[l], ln_b[l], w1[l], b1[l], w2[l], b2[l])
        return x
    x = L0_attn_x
    x = x + _layernorm(_L0_attn_ref(_layernorm(x, axis=-1), L0_attn_W_hg, L0_attn_W_out), axis=-1)
    x = x + _layernorm(_L0_ffn_ref(_layernorm(x, axis=-1), L0_ffn_wqkv, L0_ffn_q_scale, L0_ffn_k_scale, L0_ffn_wo, L0_ffn_ln_g, L0_ffn_ln_b, L0_ffn_w1, L0_ffn_b1, L0_ffn_w2, L0_ffn_b2), axis=-1)
    return x

_drawn_inputs = setup_inputs


def setup_inputs(seed=0):
    import zlib

    import numpy as np

    out = dict(_drawn_inputs(seed))
    spreads = {'L0_ffn_q_scale': (1.0, 0.6),
     'L0_ffn_k_scale': (1.0, 0.6),
     'L0_ffn_ln_g': (1.0, 0.6),
     'L0_ffn_ln_b': (0.0, 0.8),
     'L0_ffn_b1': (0.0, 0.8),
     'L0_ffn_b2': (0.0, 0.8)}
    factors = {'L0_ffn_w1': 7.473, 'L0_ffn_w2': 7.205}
    for name, (base, spread) in spreads.items():
        noise = np.random.default_rng([zlib.crc32(name.encode()), seed]).standard_normal(out[name].shape)
        drawn = base * np.exp(spread * noise) if base else spread * noise
        out[name] = jnp.asarray(drawn.astype(out[name].dtype))
    for name, factor in factors.items():
        out[name] = (out[name] * factor).astype(out[name].dtype)
    return out
```

```python
from contextlib import ExitStack

import numpy as np

import concourse.bass as bass
from concourse import mybir

F32 = mybir.dt.float32
F32R = mybir.dt.float32r
BF16 = mybir.dt.bfloat16
I32 = mybir.dt.int32
ALU = mybir.AluOpType
ACT = mybir.ActivationFunctionType
AX = mybir.AxisListType

P = 128
DIM = 128
N = 2048
HEADS, DH, WINDOW = 8, 64, 64
INNER = HEADS * DH
PAIRS = HEADS // 2
HID = int(DIM * 4 * 2 / 3)
DEPTH = 2
TILES = N // P
GT = 4
GROUPS = TILES // GT
GTOK = GT * P
LAST = DEPTH * GROUPS
CHUNKS = [(0, 128), (128, 128), (256, HID - 256)]
TAIL = HID - 256
TABW = 4 * DH
MASKED = -1.0e30
LN_EPS = 1e-5
NORM_FLOOR = 1e-24
RSQRT_SEED = 0x5F3759DF

CHAIN = {"mix": 46, 0: 67, 1: 82}


def rotary_tables():
    half = np.arange(0, DH, 2, dtype=np.float32)
    inv = (np.float32(1.0) / np.power(np.float32(10000.0), half / np.float32(DH))).astype(np.float32)
    t = np.arange(N, dtype=np.float32)
    freqs = (t[:, None] * inv[None, :]).astype(np.float32).astype(np.float64)
    base = ((half + np.float32(0.4 * DH)) / np.float32(1.4 * DH)).astype(np.float32).astype(np.float64)
    power = (t.astype(np.float64) - N // 2) / float(WINDOW // 2)
    scale = base[None, :] ** power[:, None]
    cos, sin = np.cos(freqs), np.sin(freqs)
    both = lambda a, b: np.concatenate([a, b], axis=1)
    q, k = 8.0 * scale, 1.0 / scale
    return np.concatenate([both(cos * q, cos * q), both(sin * q, -sin * q),
                           both(cos * k, cos * k), both(sin * k, -sin * k)], axis=1).astype(np.float32)


def constant_block():
    r, c = np.arange(P)[:, None], np.arange(P)[None, :]
    a = r % WINDOW
    band = (c >= a) & (c <= a + WINDOW)
    first = band & ((r >= WINDOW) | (c >= WINDOW))
    m = lambda ok: np.where(ok, 0.0, MASKED)
    return np.concatenate([np.eye(P), m(band), m(first)], axis=1).astype(np.float32)


def sandwich_kernel(nc, x, w_hg_t, w_out_t, wqkv, q_scale, k_scale, wo, ln_g, ln_b, w1, b1, w2, b2,
                    tables, consts, out):
    ctx = ExitStack()
    with ctx:
        def sb(name, shape, dt=F32):
            return ctx.enter_context(nc.sbuf_tensor(name, shape, dt))

        def sem(name):
            return ctx.enter_context(nc.semaphore(name))

        group_in = nc.dram_tensor("group_in", (LAST, 1 + GTOK, DIM), F32, kind="Internal").ap()

        def tiles_of(ap):
            return ap.rearrange("(k p) d -> p k d", p=P)

        def by_group(ap):
            return ap.rearrange("(g k p) d -> g p k d", k=GT, p=P)

        const = sb("const", [P, 3 * P])
        ident = const[:, 0:P]
        ident_bf = sb("ident_bf", [P, P], BF16)
        mask_bf = [sb(f"mask_bf{i}", [P, GT * P], BF16) for i in range(2)]
        zeros = sb("zeros", [P, P])
        w_hg_raw = sb("w_hg_raw", [P, 2 * P])
        w_hg_hi, w_hg_lo = sb("w_hg_hi", [P, 2 * P], F32R), sb("w_hg_lo", [P, 2 * P], F32R)
        w_out_sb = sb("w_out_sb", [P, P])
        wqkv_raw = [sb(f"wqkv_raw{l}", [P, 3 * INNER]) for l in range(DEPTH)]
        wqkv_hi = [sb(f"wqkv_hi{l}", [P, 3 * INNER], F32R) for l in range(DEPTH)]
        w1_raw = [sb(f"w1_raw{l}", [P, 2 * HID]) for l in range(DEPTH)]
        w1_hi = [sb(f"w1_hi{l}", [P, 2 * HID], F32R) for l in range(DEPTH)]
        wqkv_lo = [sb(f"wqkv_lo{l}", [P, 3 * INNER], F32R) for l in range(DEPTH)]
        w1_lo = [sb(f"w1_lo{l}", [P, 2 * HID], F32R) for l in range(DEPTH)]
        wo_sb = [sb(f"wo_sb{l}", [P, 4, DIM]) for l in range(DEPTH)]
        w2_sb = [sb(f"w2_sb{l}", [P, 3, DIM]) for l in range(DEPTH)]
        lngb = [sb(f"lngb{l}", [P, 2]) for l in range(DEPTH)]
        b1_sb = [sb(f"b1_sb{l}", [P, 6]) for l in range(DEPTH)]
        head_scale = [sb(f"head_scale{l}", [P, TABW]) for l in range(DEPTH)]

        x_in = sb("x_in", [P, TILES, DIM])
        xn = sb("xn", [P, GT, DIM])
        xf_sb = sb("xf_sb", [P, GT, DIM])
        act_t_hi = sb("act_t_hi", [P, GTOK], F32R)
        act_t_lo = sb("act_t_lo", [P, GTOK], F32R)
        coef_a = sb("coef_a", [P, GTOK])
        sig_gate = sb("sig_gate", [P, GTOK])
        sig_hidden = sb("sig_hidden", [P, GTOK])
        value_b = sb("value_b", [P, GTOK])
        scan_h = sb("scan_h", [P, GTOK])
        scan_carry = sb("scan_carry", [P, 1])

        h_tok = sb("h_tok", [P, GT, DIM])
        x_res = sb("x_res", [P, GT, DIM])
        tab_raw = sb("tab_raw", [P, GT, TABW])
        tab = sb("tab", [P, TABW])
        sq = sb("sq", [P, 2 * INNER])
        ss = sb("ss", [P, 2 * HEADS])
        rn = sb("rn", [P, 2 * HEADS])
        nw_x, nw_t = sb("nw_x", [P, 2 * HEADS]), sb("nw_t", [P, 2 * HEADS])
        rot_cos = sb("rot_cos", [P, 2 * HEADS, DH])
        rot_sin = sb("rot_sin", [P, 2 * HEADS, DH])
        rot = sb("rot", [P, 2 * HEADS, DH])
        q_even = sb("q_even", [P, PAIRS, P])
        q_odd = sb("q_odd", [P, PAIRS, P])
        k_t = [sb(f"k_t{i}", [P, PAIRS, WINDOW + P]) for i in range(2)]
        v_tok = [sb(f"v_tok{i}", [P, INNER]) for i in range(GT)]
        v_mid = [sb(f"v_mid{i}", [P, INNER]) for i in range(GT)]
        neg_max = [sb(f"neg_max{i}", [P, HEADS]) for i in range(2)]
        row_sum = [sb(f"row_sum{i}", [P, HEADS]) for i in range(2)]
        inv_sum = sb("inv_sum", [P, HEADS])
        probs = sb("probs", [P, HEADS, P])
        probs_t = sb("probs_t", [P, HEADS, P])
        o_tok = sb("o_tok", [P, INNER])
        o_t = sb("o_t", [P, 4, P])
        x_attn = sb("x_attn", [P, GT + 1, DIM])
        x_early = sb("x_early", [P, DIM])
        h2 = sb("h2", [P, GT, DIM])
        h2_t = sb("h2_t", [P, GTOK])
        h2_hi, h2_lo = sb("h2_hi", [P, GTOK], F32R), sb("h2_lo", [P, GTOK], F32R)
        gelu_g = sb("gelu_g", [P, 3, GTOK])
        gated = sb("gated", [P, 3, GTOK])
        y = sb("y", [P, GT, DIM])
        y_out = sb("y_out", [P, GT, DIM])
        stats = sb("stats", [P, GT, 6])
        mean_var = sb("mean_var", [P, GT, 2])
        ln_x, ln_t, ln_r = sb("ln_x", [P, GT]), sb("ln_t", [P, GT]), sb("ln_r", [P, GT])

        bank = [ctx.enter_context(nc.psum_tensor(f"bank{i}", [P, 512], F32)) for i in range(8)]
        q_bank, k_bank, v_bank = bank[0], bank[1], bank[2]
        qt_bank, kt_bank = bank[3], bank[4]
        s_bank = bank[5:7]
        misc_bank = bank[7]
        pt_bank = [bank[3], bank[4]]
        o_bank = bank[2]
        up_bank = [(bank[3], bank[4]), (bank[0], bank[1]), (bank[3], bank[4])]
        y_bank = bank[5]

        init_done = sem("init_done")
        consts_in, w_mix_in, w_ffn_in = sem("consts_in"), sem("w_mix_in"), sem("w_ffn_in")
        x_first_in, x_rest_in = sem("x_first_in"), sem("x_rest_in")
        const_bf, w_mix_split, w_split = sem("const_bf"), sem("w_mix_split"), sem("w_split")
        zero_row, zeros_ready = sem("zero_row"), sem("zeros_ready")
        w_mix_high, w_high = sem("w_mix_high"), sem("w_high")
        xn_ready, xnt_done, xnt_hi, xnt_lo = sem("xn_ready"), sem("xnt_done"), sem("xnt_hi"), sem("xnt_lo")
        hg_done, sig_done, scan_done = sem("hg_done"), sem("sig_done"), sem("scan_done")
        mixed, mix_done, early_moved = sem("mixed"), sem("mix_done"), sem("early_moved")
        xf_ready, xf_stored = sem("xf_ready"), sem("xf_stored")
        h_in, tab_in = sem("h_in"), sem("tab_in")
        res_in = [sem(f"res_in{i}") for i in range(GT)]
        v_mid_in = [sem(f"v_mid_in{i}") for i in range(GT)]
        tab_ready = sem("tab_ready")
        ht_done, ht_hi, ht_lo = sem("ht_done"), sem("ht_hi"), sem("ht_lo")
        q_done, k_done, v_done = sem("q_done"), sem("k_done"), sem("v_done")
        q_rot, k_rot, squared, rn_ready = sem("q_rot"), sem("k_rot"), sem("squared"), sem("rn_ready")
        rot_added, rot_scaled = sem("rot_added"), sem("rot_scaled")
        qt_done, kt_done, q_saved, k_saved, v_saved = sem("qt_done"), sem("kt_done"), sem("q_saved"), sem("k_saved"), sem("v_saved")
        s_done, max_ready, exp_done = sem("s_done"), sem("max_ready"), sem("exp_done")
        pt_done, pt_saved0, pt_saved1 = sem("pt_done"), sem("pt_saved0"), sem("pt_saved1")
        pv_done, o_ready, ot_done, ot_saved = sem("pv_done"), sem("o_ready"), sem("ot_done"), sem("ot_saved")
        wo_done, xa_ready = sem("wo_done"), sem("xa_ready")
        h2_in, carry_in, h2_ready = sem("h2_in"), sem("carry_in"), sem("h2_ready")
        h2t_done, h2t_saved, h2_split = sem("h2t_done"), sem("h2t_saved"), sem("h2_split")
        up_done, gelu_done, gated_done = sem("up_done"), sem("gelu_done"), sem("gated_done")
        down_done, y_read, y_ready = sem("down_done"), sem("y_read"), sem("y_ready")
        out_ready, stored = sem("out_ready"), sem("stored")
        FIRST_LAYER = 32 * GROUPS
        dve_chain = sem("dve_chain")
        settled = {e.name: sem(f"settled_{e.name}") for e in (mybir.EngineType.SP, mybir.EngineType.DVE)}

        block = ctx.enter_context(nc.Block())

        def need(eng, s, value):
            if isinstance(value, int) and value <= 0:
                return
            eng.wait_ge(s, value)
            if eng.engine == mybir.EngineType.SP and not isinstance(value, int):
                settle(eng)

        def settle(eng):
            eng.sem_inc(settled[eng.engine.name], 1)

        class At:

            def __init__(self, G, j, back, layer):
                self.t = GT * G + j - back
                self.slot = (j - back) % GT
                self.par = (j - back) % 2
                if isinstance(self.t, int):
                    self.valid = 0 <= self.t < DEPTH * TILES
                    self.layer = self.t // TILES
                    self.first = self.t % TILES == 0
                else:
                    self.valid, self.layer, self.first = True, layer, False

        def in_layer(G, layer):
            return G - GROUPS * layer

        def passes(eng, body, steps=None):
            for layer in range(DEPTH):
                G0 = GROUPS * layer
                G1 = G0 + GROUPS if layer < DEPTH - 1 else LAST - 1
                body(G0, layer)
                if steps:
                    steps.enter()
                with eng.Fori(G0 + 1, G1) as G:
                    if steps:
                        steps.at(G - (G0 + 1), CHAIN[layer])
                    body(G, layer)
                if steps:
                    steps.leave(G1 - G0 - 1)
            body(LAST - 1, DEPTH - 1)
            body(LAST, DEPTH - 1)

        class Steps:

            def __init__(self, eng, s):
                self.eng, self.sem, self.base, self.n = eng, s, 0, 0

            def link(self, ins):
                ins.then_inc(self.sem, 1)
                self.n += 1
                self.eng.wait_ge(self.sem, self.base + self.n)

            def enter(self):
                self.start, self.n = self.base + self.n, 0

            def at(self, i, each):
                self.base, self.each = self.start + i * each, each

            def leave(self, times):
                assert self.n == self.each, f"a pass of the loop has {self.n} steps"
                self.base, self.n = self.start + times * self.each, 0

        @block.sync
        def _(sp):
            sp.dma_start(x_in[:, 0:GT, :], by_group(x)[0]).then_inc(x_first_in, 16)
            sp.dma_start(const[:, :], consts).then_inc(consts_in, 16)
            sp.dma_start(w_hg_raw[:, :], w_hg_t).then_inc(w_mix_in, 16)
            sp.dma_start(w_out_sb[:, :], w_out_t).then_inc(w_mix_in, 16)
            for g in range(1, GROUPS):
                sp.dma_start(x_in[:, GT * g:GT * g + GT, :], by_group(x)[g]).then_inc(x_rest_in, 16)
            for l in range(DEPTH):
                sp.dma_start(wqkv_raw[l][:, :], wqkv[l]).then_inc(w_ffn_in, 16)
                sp.dma_start(w1_raw[l][:, :], w1[l]).then_inc(w_ffn_in, 16)
                sp.dma_start(wo_sb[l][:, :, :], wo[l].rearrange("(c p) d -> p c d", p=P)).then_inc(w_ffn_in, 16)
                sp.dma_start(w2_sb[l][:, 0:2, :], w2[l][0:256].rearrange("(c p) d -> p c d", p=P)).then_inc(w_ffn_in, 16)
                sp.dma_start(w2_sb[l][0:TAIL, 2, :], w2[l][256:HID]).then_inc(w_ffn_in, 16)
                sp.dma_start(w2_sb[l][TAIL:TAIL + 1, 2, :], b2[l:l + 1]).then_inc(w_ffn_in, 16)
                sp.dma_start(lngb[l][:, 0:1], ln_g[l].rearrange("(p a) -> p a", a=1)).then_inc(w_ffn_in, 16)
                sp.dma_start(lngb[l][:, 1:2], ln_b[l].rearrange("(p a) -> p a", a=1)).then_inc(w_ffn_in, 16)
                for part in range(2):
                    for c, (c0, cn) in enumerate(CHUNKS):
                        src = b1[l][part * HID + c0:part * HID + c0 + cn].rearrange("(p a) -> p a", a=1)
                        sp.dma_start(b1_sb[l][0:cn, 3 * part + c:3 * part + c + 1], src).then_inc(w_ffn_in, 16)
                for n, scale in enumerate((q_scale, q_scale, k_scale, k_scale)):
                    sp.dma_start(head_scale[l][:, n * DH:(n + 1) * DH],
                                 scale[l:l + 1].broadcast_to([P, DH])).then_inc(w_ffn_in, 16)

            with sp.Fori(0, GROUPS) as g:
                need(sp, xf_ready, g + 1)
                sp.dma_start(tiles_of(group_in[g, 1:1 + GTOK, :]), xf_sb[:, :, :]).then_inc(xf_stored, 16)
                sp.dma_start(group_in[g + 1, 0:1, :], xf_sb[P - 1:P, GT - 1, :]).then_inc(xf_stored, 16)
            sp.wait_ge(xf_stored, 32 * GROUPS)
            sp.wait_ge(zeros_ready, 1)
            sp.dma_start(group_in[0, 0:1, :], zeros[0:1, :]).then_inc(zero_row, 16)
            sp.dma_start(group_in[GROUPS, 0:1, :], zeros[0:1, :]).then_inc(stored, 16)
            sp.wait_ge(zero_row, 16)
            sp.wait_ge(stored, 16)

            def load_group(G):
                need(sp, ht_done, G)
                sp.dma_start(h_tok[:, :, 0:64], tiles_of(group_in[G, 1:1 + GTOK, 0:64])).then_inc(h_in, 16)
                sp.dma_start(h_tok[:, :, 64:128], tiles_of(group_in[G, 0:GTOK, 64:128])).then_inc(h_in, 16)
                need(sp, tab_ready, GT * G)
                sp.dma_start(tab_raw[:, :, :], tables[G]).then_inc(tab_in, 16)

            def load_residual(G, j):
                need(sp, xa_ready, GT * (G - 1) + j + 1)
                sp.dma_start(x_res[:, j, :], group_in[G, 1 + j * P:1 + (j + 1) * P, :]).then_inc(res_in[j], 16)

            def load_h2(F):
                need(sp, xa_ready, GT * F + GT)
                need(sp, early_moved, F + 1)
                sp.dma_start(h2[0:1, :, 64:128], x_attn[P - 1:P, 0:GT, 64:128]).then_inc(h2_in, 16)
                sp.dma_start(h2[:, :, 0:64], x_attn[:, 1:GT + 1, 0:64]).then_inc(h2_in, 16)
                sp.dma_start(h2[1:113, :, 64:128], x_attn[0:112, 1:GT + 1, 64:128]).then_inc(h2_in, 16)
                sp.dma_start(h2[113:128, :, 64:128], x_attn[112:127, 1:GT + 1, 64:128]).then_inc(h2_in, 16)
                need(sp, h2_in, 64 * (F + 1))
                ends = isinstance(F, int) and F % GROUPS == GROUPS - 1
                last = zeros[P - 1:P, 64:128] if ends else x_attn[P - 1:P, GT, 64:128]
                sp.dma_start(x_attn[P - 1:P, 0, 64:128], last).then_inc(carry_in, 16)

            def store(F, layer):
                if layer == 0:
                    need(sp, y_ready, F + 1)
                    sp.dma_start(tiles_of(group_in[F + GROUPS, 1:1 + GTOK, :]), y[:, :, :]).then_inc(stored, 16)
                    if not (isinstance(F, int) and F == GROUPS - 1):
                        sp.dma_start(group_in[F + GROUPS + 1, 0:1, :], y[P - 1:P, GT - 1, :]).then_inc(stored, 16)
                else:
                    need(sp, out_ready, F - GROUPS + 1)
                    sp.dma_start(by_group(out)[F - GROUPS], y_out[:, :, :]).then_inc(stored, 16)
                need(sp, carry_in, 16 * (F + 1))

            load_group(0)
            for j in range(GT):
                load_residual(0, j)

            def body(G, layer):
                number = isinstance(G, int)
                for j in range(GT):
                    cur = At(G, j, 0, layer)
                    if cur.valid:
                        need(sp, pv_done, cur.t - 3)
                        need(sp, v_saved, cur.t + 1)
                        sp.dma_start(v_mid[j][0:64, :], v_tok[(j - 1) % GT][64:128, :]).then_inc(v_mid_in[j], 16)
                        sp.dma_start(v_mid[j][64:128, :], v_tok[j][0:64, :]).then_inc(v_mid_in[j], 16)
                    if j == 3:
                        if not (number and G == 0):
                            load_h2(G - 1)
                        if not (number and G + 1 >= LAST):
                            if layer == 0:
                                need(sp, stored, 16 + 32 * (G - 1))
                            else:
                                sp.wait_ge(stored, FIRST_LAYER - 16 if number and G == GROUPS else FIRST_LAYER)
                            load_group(G + 1)
                            load_residual(G + 1, 0)
                    elif not (number and (G == 0 or G >= LAST)):
                        load_residual(G, j + 1)
                if not (number and G == 0):
                    store(G - 1, (G - 1) // GROUPS if number else layer)

            passes(sp, body)
            sp.wait_ge(stored, FIRST_LAYER + 16 * GROUPS)

        @block.gpsimd
        def _(pool):
            pool.memset(zeros[:, :], 0.0).then_inc(zeros_ready, 1)
            pool.memset(q_even[:, :, :], 0.0).then_inc(init_done, 1)
            pool.memset(q_odd[:, :, :], 0.0).then_inc(init_done, 1)
            pool.memset(k_t[0][:, :, 0:WINDOW], 0.0).then_inc(init_done, 1)
            pool.memset(v_tok[GT - 1][:, :], 0.0).then_inc(init_done, 1)
            pool.memset(x_attn[:, 0, :], 0.0).then_inc(init_done, 1)
            pool.memset(gated[:, 2, :], 1.0).then_inc(init_done, 1)
            pool.wait_ge(w_mix_high, 1)
            pool.tensor_tensor(w_hg_lo[:, :], w_hg_raw[:, :], w_hg_hi[:, :].bitcast(F32), ALU.subtract).then_inc(w_mix_split, 1)
            for l in range(DEPTH):
                pool.wait_ge(w_high, 2 * l + 2)
                pool.tensor_tensor(wqkv_lo[l][:, :], wqkv_raw[l][:, :], wqkv_hi[l][:, :].bitcast(F32), ALU.subtract).then_inc(w_split, 1)
                pool.tensor_tensor(w1_lo[l][:, :], w1_raw[l][:, :], w1_hi[l][:, :].bitcast(F32), ALU.subtract).then_inc(w_split, 1)

            def scale_table(G, j, layer):
                pool.wait_ge(tab_in, 16 * (G + 1))
                need(pool, k_rot, 2 * (GT * G + j))
                pool.tensor_tensor(tab[:, :], tab_raw[:, j, :], head_scale[layer][:, :], ALU.mult).then_inc(tab_ready, 1)

            def body(G, layer):
                number = isinstance(G, int)
                if number and G >= LAST:
                    return
                for j in range(GT):
                    t = GT * G + j
                    scale_table(G, j, layer)
                    pool.wait_ge(k_rot, 2 * (t + 1))
                    need(pool, kt_done, t)
                    pool.tensor_tensor(rot[:, :, 0:32], rot_cos[:, :, 0:32], rot_sin[:, :, 32:64], ALU.add).then_inc(rot_added, 1)
                    pool.tensor_tensor(rot[:, :, 32:64], rot_cos[:, :, 32:64], rot_sin[:, :, 0:32], ALU.add).then_inc(rot_added, 1)
                    pool.wait_ge(rn_ready, t + 1)
                    pool.wait_ge(rot_added, 2 * (t + 1))
                    pool.tensor_tensor(rot[:, :, :], rot[:, :, :], rn[:, :].unsqueeze(2).broadcast_to([P, 2 * HEADS, DH]),
                                       ALU.mult).then_inc(rot_scaled, 1)
            passes(pool, body)

        W_IN = 16 * DEPTH * 18

        @block.tensor
        def _(pe):
            def product3(out_ap, lhs, rhs, lhs_lo, rhs_lo):
                pe.matmul(out_ap, lhs, rhs, start=True, stop=False)
                pe.matmul(out_ap, lhs, rhs_lo, start=False, stop=False)
                return pe.matmul(out_ap, lhs_lo, rhs, start=False, stop=True)

            def mixer(g):
                pe.wait_ge(xn_ready, g + 1)
                need(pe, xnt_lo, g)
                for k in range(GT):
                    last = pe.transpose(qt_bank[:, k * P:(k + 1) * P], xn[:, k, :], ident)
                last.then_inc(xnt_done, 1)
                pe.wait_ge(xnt_hi, g + 1)
                pe.wait_ge(xnt_lo, g + 1)
                need(pe, scan_done, g)
                for n, b in enumerate((q_bank, k_bank)):
                    cols = slice(n * P, (n + 1) * P)
                    product3(b[:, :], w_hg_hi[:, cols], act_t_hi[:, :], w_hg_lo[:, cols], act_t_lo[:, :]).then_inc(hg_done, 1)
                pe.wait_ge(scan_done, g + 1)
                need(pe, mix_done, g)
                for k in range(GT):
                    last = pe.matmul(v_bank[:, k * P:(k + 1) * P], scan_h[:, k * P:(k + 1) * P], w_out_sb[:, :],
                                     start=True, stop=True)
                last.then_inc(mixed, 1)

            pe.wait_ge(consts_in, 16)
            pe.wait_ge(w_mix_in, 32)
            pe.wait_ge(w_mix_high, 1)
            pe.wait_ge(w_mix_split, 1)
            mixer(0)
            with pe.Fori(1, GROUPS) as g:
                mixer(g)
            pe.wait_ge(mix_done, GROUPS)

            def transpose_inputs(G):
                pe.wait_ge(h_in, 32 * (G + 1))
                need(pe, xa_ready, GT * (G - 1) + 1)
                for k in range(GT):
                    last = pe.transpose(misc_bank[:, k * P:(k + 1) * P], h_tok[:, k, :], ident)
                last.then_inc(ht_done, 1)

            def transpose_qk(a):
                pe.wait_ge(rot_scaled, a.t + 1)
                for half, (b, ready) in enumerate(((qt_bank, qt_done), (kt_bank, kt_done))):
                    for p in range(PAIRS):
                        h = half * HEADS + 2 * p
                        last = pe.transpose(b[:, p * P:(p + 1) * P], rot[:, h:h + 2, :].rearrange("p h d -> p (h d)"), ident)
                    last.then_inc(ready, 1)

            def transpose_o(a):
                pe.wait_ge(o_ready, a.t + 1)
                for c in range(4):
                    last = pe.transpose(misc_bank[:, c * P:(c + 1) * P], o_tok[:, c * P:(c + 1) * P], ident)
                last.then_inc(ot_done, 1)

            def project_qkv(a, G):
                pe.wait_ge(ht_hi, G + 1)
                pe.wait_ge(ht_lo, G + 1)
                need(pe, q_rot, 2 * a.t)
                need(pe, k_rot, 2 * a.t)
                need(pe, squared, 2 * a.t)
                need(pe, v_saved, a.t)
                need(pe, o_ready, a.t - 2)
                tok = slice(a.slot * P, (a.slot + 1) * P)
                for n, (b, ready) in enumerate(((q_bank, q_done), (k_bank, k_done), (v_bank, v_done))):
                    w = slice(n * INNER, (n + 1) * INNER)
                    product3(b[:, :], act_t_hi[:, tok], wqkv_hi[a.layer][:, w],
                             act_t_lo[:, tok], wqkv_lo[a.layer][:, w]).then_inc(ready, 1)

            def transpose_probs(a):
                for half in range(2):
                    pe.wait_ge(exp_done, 2 * a.t + 1 + half)
                    if half == 0:
                        pe.wait_ge(q_saved, 2 * min_next(a))
                        pe.wait_ge(k_saved, 2 * min_next(a))
                    for h in range(4 * half, 4 * half + 4):
                        last = pe.transpose(pt_bank[half][:, (h % 4) * P:(h % 4 + 1) * P], probs[:, h, :], ident)
                    last.then_inc(pt_done, 1)

            def min_next(a):
                return min(a.t + 2, DEPTH * TILES) if isinstance(a.t, int) else a.t + 2

            def project_out(a):
                pe.wait_ge(ot_saved, a.t + 1)
                for c in range(4):
                    last = pe.matmul(misc_bank[:, 0:DIM], o_t[:, c, :], wo_sb[a.layer][:, c, :],
                                     start=(c == 0), stop=(c == 3))
                last.then_inc(wo_done, 1)

            def scores(a, half):
                if half == 0:
                    pe.wait_ge(q_saved, 2 * (a.t + 1))
                    pe.wait_ge(k_saved, 2 * (a.t + 1))
                need(pe, exp_done, 2 * (a.t - 1) + 1 + half if not (isinstance(a.t, int) and a.t == 0) else 0)
                b = s_bank[half]
                pe.matmul(b[:, :], ident_bf[:, :], mask_bf[1 if a.first else 0][:, :], start=True, stop=True)
                for h in range(4 * half, 4 * half + 4):
                    q, col = (q_even, q_odd)[h % 2][:, h // 2, :], (h % 4) * P
                    keys = k_t[a.par][:, h // 2, :]
                    for low in (0, 64):
                        last = pe.matmul(b[low:low + 64, col:col + P], q[:, low:low + 64], keys[:, low:low + P],
                                         start=False, stop=True, skip_group_check=True)
                last.then_inc(s_done, 1)

            def mix_values(a, G):
                group = (a.t - a.slot) // GT if isinstance(a.t, int) else group_of(a, G)
                pe.wait_ge(pt_saved0, a.t + 1)
                pe.wait_ge(pt_saved1, a.t + 1)
                pe.wait_ge(v_mid_in[a.slot], 32 * (group + 1))
                need(pe, v_saved, min_next(a) + (0 if isinstance(a.t, int) and a.t + 2 >= DEPTH * TILES else 1))
                for h in range(HEADS):
                    cols = slice(h * DH, (h + 1) * DH)
                    for low, v in ((0, v_mid[a.slot]), (64, v_tok[a.slot])):
                        last = pe.matmul(o_bank[low:low + 64, cols], probs_t[:, h, low:low + 64], v[:, cols],
                                         start=True, stop=True)
                last.then_inc(pv_done, 1)

            def group_of(a, G):
                return G if a.slot < 2 else G - 1

            def transpose_h2(F):
                pe.wait_ge(h2_ready, F + 1)
                if isinstance(F, int) and F + 2 >= LAST:
                    pe.wait_ge(xa_ready, min(GT * (F + 1) + 1, DEPTH * TILES))
                else:
                    pe.wait_ge(ht_lo, F + 3)
                for k in range(GT):
                    last = pe.transpose(misc_bank[:, k * P:(k + 1) * P], h2[:, k, :], ident)
                last.then_inc(h2t_done, 1)

            def feed_forward(F, layer, t_now):
                pe.wait_ge(h2_split, F + 1)
                pe.wait_ge(q_rot, 2 * t_now)
                pe.wait_ge(k_rot, 2 * t_now)
                pe.wait_ge(squared, 2 * t_now)
                for c, (c0, cn) in enumerate(CHUNKS):
                    if c == 2:
                        pe.wait_ge(gated_done, 3 * F + 1)
                    for part, b in enumerate(up_bank[c]):
                        w = slice(part * HID + c0, part * HID + c0 + cn)
                        last = product3(b[0:cn, :], w1_hi[layer][:, w], h2_hi[:, :], w1_lo[layer][:, w], h2_lo[:, :])
                    last.then_inc(up_done, 1)
                pe.wait_ge(gated_done, 3 * F + 3)
                for k in range(GT):
                    for c, (c0, cn) in enumerate(CHUNKS):
                        rows = cn + 1 if c == 2 else cn
                        last = pe.matmul(y_bank[:, k * P:(k + 1) * P], gated[0:rows, c, k * P:(k + 1) * P],
                                         w2_sb[layer][0:rows, c, :], start=(c == 0), stop=(c == 2))
                last.then_inc(down_done, 1)

            pe.wait_ge(init_done, 6)
            pe.wait_ge(const_bf, 3)
            pe.wait_ge(w_ffn_in, W_IN)
            pe.wait_ge(w_high, 4)
            pe.wait_ge(w_split, 4)
            transpose_inputs(0)

            def body(G, layer):
                number = isinstance(G, int)
                for j in range(GT):
                    cur, prev, mid, done = (At(G, j, back, layer) for back in range(4))
                    if prev.valid:
                        transpose_qk(prev)
                    if done.valid:
                        transpose_o(done)
                    if cur.valid:
                        project_qkv(cur, G)
                    if mid.valid:
                        transpose_probs(mid)
                    if done.valid:
                        project_out(done)
                    if prev.valid:
                        if j == 0 and not (number and G < 2):
                            pe.wait_ge(early_moved, G)
                        scores(prev, 0)
                    if j == 3 and not (number and G + 1 >= LAST):
                        transpose_inputs(G + 1) if not (number and G == 0) else transpose_inputs(G + 1)
                    if prev.valid:
                        scores(prev, 1)
                    ffn = j == 3 and not (number and G == 0)
                    if ffn:
                        transpose_h2(G - 1)
                    if mid.valid:
                        mix_values(mid, G)
                    if ffn:
                        t_now = min(GT * G + GT, DEPTH * TILES) if number else GT * G + GT
                        need(pe, exp_done, 2 * (t_now - 1) - 1 + (2 if number and G == LAST else 0))
                        feed_forward(G - 1, (G - 1) // GROUPS if number else layer, t_now)

            passes(pe, body)

        @block.scalar
        def _(act):
            act.wait_ge(w_mix_in, 32)
            act.copy(w_hg_hi[:, :], w_hg_raw[:, :]).then_inc(w_mix_high, 1)

            def mixer(g):
                act.wait_ge(xnt_done, g + 1)
                need(act, hg_done, 2 * g)
                act.copy(act_t_hi[:, :], qt_bank[:, :]).then_inc(xnt_hi, 1)
                act.wait_ge(hg_done, 2 * g + 2)
                need(act, scan_done, g)
                act.activation(sig_hidden[:, :], q_bank[:, :], ACT.Sigmoid).then_inc(sig_done, 1)
                act.activation(sig_gate[:, :], k_bank[:, :], ACT.Sigmoid).then_inc(sig_done, 1)
                act.activation(coef_a[:, :], k_bank[:, :], ACT.Sigmoid, scale=-1.0).then_inc(sig_done, 1)

            mixer(0)
            with act.Fori(1, GROUPS) as g:
                mixer(g)
            act.wait_ge(w_ffn_in, W_IN)
            for l in range(DEPTH):
                act.copy(wqkv_hi[l][:, :], wqkv_raw[l][:, :]).then_inc(w_high, 1)
                act.copy(w1_hi[l][:, :], w1_raw[l][:, :]).then_inc(w_high, 1)
            act.wait_ge(hg_done, 2 * GROUPS)

            def save_inputs(G):
                act.wait_ge(ht_done, G + 1)
                need(act, v_done, GT * G)
                act.copy(act_t_hi[:, :], misc_bank[:, :]).then_inc(ht_hi, 1)

            save_inputs(0)

            def exponentials(a, half):
                act.wait_ge(max_ready, 2 * a.t + 1 + half)
                if half == 0:
                    need(act, pt_done, 2 * a.t)
                    need(act, o_ready, a.t - 1)
                for h in range(4 * half, 4 * half + 4):
                    last = act.activation(probs[:, h, :], s_bank[half][:, (h % 4) * P:(h % 4 + 1) * P], ACT.Exp,
                                          bias=neg_max[a.par][:, h:h + 1], accum_out=row_sum[a.par][:, h:h + 1])
                last.then_inc(exp_done, 1)

            def body(G, layer):
                number = isinstance(G, int)
                for j in range(GT):
                    cur, prev, mid, done = (At(G, j, back, layer) for back in range(4))
                    if prev.valid:
                        act.wait_ge(qt_done, prev.t + 1)
                        need(act, s_done, 2 * prev.t)
                        act.copy(q_even[0:64, :, :], qt_bank[0:64, :].rearrange("p (c t) -> p c t", c=PAIRS)).then_inc(q_saved, 1)
                        act.copy(q_odd[64:128, :, :], qt_bank[64:128, :].rearrange("p (c t) -> p c t", c=PAIRS)).then_inc(q_saved, 1)
                    if done.valid:
                        act.wait_ge(ot_done, done.t + 1)
                        need(act, wo_done, done.t)
                        act.copy(o_t[:, :, :], misc_bank[:, :].rearrange("p (c t) -> p c t", c=4)).then_inc(ot_saved, 1)
                    if cur.valid:
                        need(act, rn_ready, cur.t)
                        for n, (b, ready) in enumerate(((q_bank, q_done), (k_bank, k_done))):
                            act.wait_ge(ready, cur.t + 1)
                            act.activation(sq[:, n * INNER:(n + 1) * INNER], b[:, :], ACT.Square).then_inc(squared, 1)
                        act.wait_ge(v_done, cur.t + 1)
                        need(act, pv_done, cur.t - 3)
                        if not (number and G == 0):
                            slot = (j - 3) % GT
                            act.wait_ge(v_mid_in[slot], 32 * (G + 1 if j == 3 else G))
                        act.copy(v_tok[j][:, :], v_bank[:, :]).then_inc(v_saved, 1)
                    if mid.valid:
                        act.wait_ge(pt_done, 2 * mid.t + 1)
                        need(act, pv_done, mid.t)
                        act.copy(probs_t[:, 0:4, :], pt_bank[0][:, :].rearrange("p (h t) -> p h t", h=4)).then_inc(pt_saved0, 1)
                    if prev.valid:
                        exponentials(prev, 0)
                    if j == 3 and not (number and G + 1 >= LAST):
                        save_inputs(G + 1)
                    if prev.valid:
                        exponentials(prev, 1)
                    if j == 3 and not (number and G == 0):
                        F = G - 1
                        l = F // GROUPS if number else layer
                        act.wait_ge(h2t_done, F + 1)
                        act.activation(h2_t[:, :], misc_bank[:, :], ACT.Identity, bias=lngb[l][:, 1:2],
                                       scale=lngb[l][:, 0:1]).then_inc(h2t_saved, 1)
                        for c, (c0, cn) in enumerate(CHUNKS):
                            act.wait_ge(up_done, 3 * F + c + 1)
                            act.activation(gelu_g[0:cn, c, :], up_bank[c][1][0:cn, :], ACT.Gelu,
                                           bias=b1_sb[l][0:cn, 3 + c:4 + c]).then_inc(gelu_done, 1)

            passes(act, body)

        @block.vector
        def _(dve):
            steps = Steps(dve, dve_chain)
            link = steps.link

            def rsqrt(out_ap, x_ap, half_ap, tmp):
                link(dve.tensor_scalar(out_ap.bitcast(I32), x_ap.bitcast(I32), -0.5, float(RSQRT_SEED), ALU.mult, ALU.add))
                link(dve.tensor_scalar(half_ap, x_ap, -0.5, None, ALU.mult))
                for n in range(3):
                    link(dve.tensor_tensor(tmp, out_ap, out_ap, ALU.mult))
                    link(dve.tensor_tensor(tmp, tmp, half_ap, ALU.mult))
                    last = dve.scalar_tensor_tensor(out_ap, tmp, 1.5, out_ap, ALU.add, ALU.mult)
                    if n < 2:
                        link(last)
                return last

            def moments(src):
                settle(dve)
                for k in range(GT):
                    last = dve.bn_stats(stats[:, k, :], src(k))
                link(last)
                settle(dve)
                for k in range(GT):
                    last = dve.bn_aggr(mean_var[:, k, :], stats[:, k, :])
                link(last)
                link(dve.tensor_scalar(ln_x[:, :], mean_var[:, :, 1], LN_EPS, None, ALU.add))
                link(rsqrt(ln_r[:, :], ln_x[:, :], ln_x[:, :], ln_t[:, :]))

            def normalise(dst, src):
                for k in range(GT):
                    last = dve.tensor_scalar(dst(k), src(k), mean_var[:, k, 0:1], ln_r[:, k:k + 1], ALU.subtract, ALU.mult)
                return last

            dve.wait_ge(consts_in, 16)
            dve.tensor_copy(ident_bf[:, :], ident).then_inc(const_bf, 1)
            for n, m in enumerate(mask_bf):
                src = const[:, (n + 1) * P:(n + 2) * P]
                dve.tensor_copy(m[:, :].rearrange("p (h k) -> p h k", h=GT),
                                src.unsqueeze(1).broadcast_to([P, GT, P])).then_inc(const_bf, 1)

            def mixer(g, carry):
                tile = lambda k: x_in[:, GT * g + k, :]
                moments(tile)
                need(dve, xnt_done, g)
                normalise(lambda k: xn[:, k, :], tile).then_inc(xn_ready, 1)
                dve.wait_ge(xnt_hi, g + 1)
                dve.tensor_tensor(act_t_lo[:, :], qt_bank[:, :], act_t_hi[:, :].bitcast(F32), ALU.subtract).then_inc(xnt_lo, 1)
                dve.wait_ge(sig_done, 3 * g + 3)
                link(dve.tensor_scalar(sig_hidden[:, :], sig_hidden[:, :], 0.5, None, ALU.min))
                link(dve.scalar_tensor_tensor(value_b[:, :], q_bank[:, :], 0.0, sig_hidden[:, :], ALU.max, ALU.add))
                link(dve.tensor_tensor(value_b[:, :], value_b[:, :], sig_gate[:, :], ALU.mult))
                need(dve, mixed, g)
                dve.tensor_tensor_scan(scan_h[:, :], coef_a[:, :], value_b[:, :], scan_carry[:, 0:1] if carry else 0.0,
                                       ALU.mult, ALU.add).then_inc(scan_done, 1)
                dve.wait_ge(scan_done, g + 1)
                dve.tensor_copy(scan_carry[:, :], scan_h[:, GTOK - 1:GTOK])
                dve.wait_ge(mixed, g + 1)
                out_k = lambda k: v_bank[:, k * P:(k + 1) * P]
                moments(out_k)
                last = normalise(lambda k: y[:, k, :], out_k)
                last.then_inc(mix_done, 1)
                dve.wait_ge(mix_done, g + 1)
                group = x_in[:, bass.ds(GT * g, GT), :] if not isinstance(g, int) else x_in[:, GT * g:GT * g + GT, :]
                link(dve.tensor_tensor(group, group, y[:, :, :], ALU.add))
                moments(tile)
                need(dve, xf_stored, 32 * g)
                normalise(lambda k: xf_sb[:, k, :], tile).then_inc(xf_ready, 1)

            dve.wait_ge(x_first_in, 16)
            mixer(0, False)
            dve.wait_ge(x_rest_in, 16 * (GROUPS - 1))
            steps.enter()
            with dve.Fori(1, GROUPS) as g:
                steps.at(g - 1, CHAIN["mix"])
                mixer(g, True)
            steps.leave(GROUPS - 1)

            def split_inputs(G):
                dve.wait_ge(ht_hi, G + 1)
                need(dve, v_done, GT * G)
                dve.tensor_tensor(act_t_lo[:, :], misc_bank[:, :], act_t_hi[:, :].bitcast(F32), ALU.subtract).then_inc(ht_lo, 1)

            split_inputs(0)

            def save_k(a):
                dve.wait_ge(kt_done, a.t + 1)
                need(dve, s_done, 2 * a.t)
                src = kt_bank[:, :].rearrange("p (c t) -> p c t", c=PAIRS)
                dve.tensor_copy(k_t[a.par][:, :, WINDOW:WINDOW + P], src).then_inc(k_saved, 1)
                carried = k_t[1 - a.par][:, :, 0:WINDOW]
                if isinstance(a.t, int) and a.t % TILES == TILES - 1:
                    dve.memset(carried, 0.0).then_inc(k_saved, 1)
                else:
                    dve.tensor_copy(carried, src[:, :, WINDOW:P]).then_inc(k_saved, 1)

            def rotate(a):
                dve.wait_ge(tab_ready, a.t + 1)
                need(dve, rot_added, 2 * a.t)
                for n, (b, done) in enumerate(((q_bank, q_rot), (k_bank, k_rot))):
                    dve.wait_ge(squared, 2 * a.t + 1 + n)
                    src = b[:, :].rearrange("p (h d) -> p h d", h=HEADS)
                    for m, dst in enumerate((rot_cos, rot_sin)):
                        table = tab[:, (2 * n + m) * DH:(2 * n + m + 1) * DH]
                        dve.tensor_tensor(dst[:, n * HEADS:(n + 1) * HEADS, :], src,
                                          table.unsqueeze(1).broadcast_to([P, HEADS, DH]), ALU.mult).then_inc(done, 1)

            def inverse_norms(a):
                link(dve.tensor_reduce(ss[:, :], sq[:, :].rearrange("p (h d) -> p h d", h=2 * HEADS), AX.X, ALU.add))
                link(dve.tensor_scalar(nw_x[:, :], ss[:, :], NORM_FLOOR, None, ALU.max))
                need(dve, rot_scaled, a.t)
                rsqrt(rn[:, :], nw_x[:, :], nw_x[:, :], nw_t[:, :]).then_inc(rn_ready, 1)

            def add_residual(a, G):
                group = G if a.slot == 0 else G - 1
                dve.wait_ge(wo_done, a.t + 1)
                dve.wait_ge(res_in[a.slot], 16 * (group + 1))
                dst = x_early[:, :] if a.slot == 0 else x_attn[:, a.slot + 1, :]
                dve.tensor_tensor(dst, misc_bank[:, 0:DIM], x_res[:, a.slot, :], ALU.add).then_inc(xa_ready, 1)

            def row_max(a, half):
                dve.wait_ge(s_done, 2 * a.t + 1 + half)
                need(dve, exp_done, 2 * (a.t - 1))
                src = s_bank[half][:, :].rearrange("p (h k) -> p h k", h=4)
                dve.tensor_reduce(neg_max[a.par][:, 4 * half:4 * half + 4], src, AX.X, ALU.max, negate=True).then_inc(max_ready, 1)

            def divide_o(a):
                dve.wait_ge(exp_done, 2 * a.t + 2)
                link(dve.reciprocal(inv_sum[:, :], row_sum[a.par][:, :]))
                dve.wait_ge(pv_done, a.t + 1)
                need(dve, ot_done, a.t)
                dve.tensor_tensor(o_tok[:, :].rearrange("p (h d) -> p h d", h=HEADS),
                                  o_bank[:, :].rearrange("p (h d) -> p h d", h=HEADS),
                                  inv_sum[:, :].unsqueeze(2).broadcast_to([P, HEADS, DH]), ALU.mult).then_inc(o_ready, 1)

            def layer_norm_h2(F):
                dve.wait_ge(h2_in, 64 * (F + 1))
                tile = lambda k: h2[:, k, :]
                moments(tile)
                normalise(tile, tile).then_inc(h2_ready, 1)

            def split_h2(F):
                dve.wait_ge(h2t_saved, F + 1)
                link(dve.tensor_copy(h2_hi[:, :], h2_t[:, :]))
                dve.tensor_tensor(h2_lo[:, :], h2_t[:, :], h2_hi[:, :].bitcast(F32), ALU.subtract).then_inc(h2_split, 1)

            def gate(F, layer, c, cn):
                dve.wait_ge(gelu_done, 3 * F + c + 1)
                dve.scalar_tensor_tensor(gated[0:cn, c, :], up_bank[c][0][0:cn, :], b1_sb[layer][0:cn, c:c + 1],
                                         gelu_g[0:cn, c, :], ALU.add, ALU.mult).then_inc(gated_done, 1)

            def finish_group(F, layer, early):
                dve.wait_ge(down_done, F + 1)
                dve.wait_ge(stored, 16 + 32 * F if layer == 0 else FIRST_LAYER)
                add = dve.tensor_tensor(y[:, :, :], y_bank[:, :].rearrange("p (k d) -> p k d", k=GT),
                                        x_attn[:, 1:GT + 1, :], ALU.add)
                add.then_inc(y_read, 1)
                dve.wait_ge(y_read, F + 1)
                dve.wait_ge(carry_in, 16 * (F + 1))
                if early:
                    dve.wait_ge(xa_ready, GT * (F + 1) + 1)
                    dve.tensor_copy(x_attn[:, 1, :], x_early[:, :]).then_inc(early_moved, 1)
                if layer == 0:
                    dve.nop().then_inc(y_ready, 1)
                else:
                    g = F - GROUPS
                    tile = lambda k: y[:, k, :]
                    moments(tile)
                    dve.wait_ge(stored, FIRST_LAYER + 16 * g)
                    link(normalise(lambda k: y_out[:, k, :], tile))
                    group = x_in[:, GT * g:GT * g + GT, :] if isinstance(g, int) else x_in[:, bass.ds(GT * g, GT), :]
                    dve.tensor_tensor(y_out[:, :, :], y_out[:, :, :], group, ALU.add).then_inc(out_ready, 1)

            def body(G, layer):
                number = isinstance(G, int)
                for j in range(GT):
                    cur, prev, mid, done = (At(G, j, back, layer) for back in range(4))
                    ffn = j == 3 and not (number and G == 0)
                    if prev.valid:
                        save_k(prev)
                    if cur.valid:
                        rotate(cur)
                    if ffn:
                        layer_norm_h2(G - 1)
                    if mid.valid:
                        dve.wait_ge(pt_done, 2 * mid.t + 2)
                        need(dve, pv_done, mid.t)
                        dve.tensor_copy(probs_t[:, 4:8, :], pt_bank[1][:, :].rearrange("p (h t) -> p h t", h=4)).then_inc(pt_saved1, 1)
                    if cur.valid:
                        inverse_norms(cur)
                    if done.valid:
                        add_residual(done, G)
                    if prev.valid:
                        row_max(prev, 0)
                    if j == 3 and not (number and G + 1 >= LAST):
                        split_inputs(G + 1)
                    if prev.valid:
                        row_max(prev, 1)
                    if ffn:
                        split_h2(G - 1)
                    if mid.valid:
                        divide_o(mid)
                    if ffn:
                        l = (G - 1) // GROUPS if number else layer
                        for c, (c0, cn) in enumerate(CHUNKS):
                            gate(G - 1, l, c, cn)
                        finish_group(G - 1, l, not (number and G >= LAST))
                    elif j == 3:
                        dve.wait_ge(xa_ready, 1)
                        dve.tensor_copy(x_attn[:, 1, :], x_early[:, :]).then_inc(early_moved, 1)

            passes(dve, body, steps)


def kernel(L0_attn_x, L0_attn_W_hg, L0_attn_W_out, L0_ffn_wqkv, L0_ffn_q_scale, L0_ffn_k_scale, L0_ffn_wo,
           L0_ffn_ln_g, L0_ffn_ln_b, L0_ffn_w1, L0_ffn_b1, L0_ffn_w2, L0_ffn_b2):
    import concourse.bacc as bacc
    from concourse.bass_utils import run_bass_kernel_spmd

    tables = np.tile(rotary_tables().reshape(GROUPS, GT, P, TABW).transpose(0, 2, 1, 3), (DEPTH, 1, 1, 1))
    arrays = {
        "x": np.asarray(L0_attn_x).reshape(N, DIM),
        "w_hg_t": np.asarray(L0_attn_W_hg).T,
        "w_out_t": np.asarray(L0_attn_W_out).T,
        "wqkv": L0_ffn_wqkv, "q_scale": L0_ffn_q_scale, "k_scale": L0_ffn_k_scale, "wo": L0_ffn_wo,
        "ln_g": L0_ffn_ln_g, "ln_b": L0_ffn_ln_b, "w1": L0_ffn_w1, "b1": L0_ffn_b1, "w2": L0_ffn_w2,
        "b2": L0_ffn_b2, "tables": tables, "consts": constant_block(),
    }
    arrays = {k: np.ascontiguousarray(v) for k, v in arrays.items()}
    nc = bacc.Bacc("TRN2", target_bir_lowering=False, num_devices=1)
    args = [nc.dram_tensor(k, a.shape, mybir.dt.from_np(a.dtype), kind="ExternalInput").ap() for k, a in arrays.items()]
    out = nc.dram_tensor("out", (N, DIM), F32, kind="ExternalOutput").ap()
    sandwich_kernel(nc, *args, out)
    r = run_bass_kernel_spmd(nc, [arrays], core_ids=[0])
    return r.results[0]["out"].reshape(1, N, DIM)
```

```python
from contextlib import ExitStack

import numpy as np

import concourse.bass as bass
from concourse import mybir

F32 = mybir.dt.float32
F32R = mybir.dt.float32r
BF16 = mybir.dt.bfloat16
I32 = mybir.dt.int32
ALU = mybir.AluOpType
ACT = mybir.ActivationFunctionType
AX = mybir.AxisListType

P = 128
DIM = 128
N = 2048
HEADS, DH, WINDOW = 8, 64, 64
INNER = HEADS * DH
PAIRS = HEADS // 2
HID = int(DIM * 4 * 2 / 3)
DEPTH = 2
TILES = N // P
GT = 4
GROUPS = TILES // GT
GTOK = GT * P
LAST = DEPTH * GROUPS
CHUNKS = [(0, 128), (128, 128), (256, HID - 256)]
TAIL = HID - 256
TABW = 4 * DH
MASKED = -1.0e30
LN_EPS = 1e-5
NORM_FLOOR = 1e-24
RSQRT_SEED = 0x5F3759DF

CHAIN = {"mix": 46, 0: 51, 1: 66}


def rotary_tables():
    half = np.arange(0, DH, 2, dtype=np.float32)
    inv = (np.float32(1.0) / np.power(np.float32(10000.0), half / np.float32(DH))).astype(np.float32)
    t = np.arange(N, dtype=np.float32)
    freqs = (t[:, None] * inv[None, :]).astype(np.float32).astype(np.float64)
    base = ((half + np.float32(0.4 * DH)) / np.float32(1.4 * DH)).astype(np.float32).astype(np.float64)
    power = (t.astype(np.float64) - N // 2) / float(WINDOW // 2)
    scale = base[None, :] ** power[:, None]
    cos, sin = np.cos(freqs), np.sin(freqs)
    both = lambda a, b: np.concatenate([a, b], axis=1)
    q, k = 8.0 * scale, 1.0 / scale
    return np.concatenate([both(cos * q, cos * q), both(sin * q, -sin * q),
                           both(cos * k, cos * k), both(sin * k, -sin * k)], axis=1).astype(np.float32)


def constant_block():
    r, c = np.arange(P)[:, None], np.arange(P)[None, :]
    a = r % WINDOW
    band = (c >= a) & (c <= a + WINDOW)
    first = band & ((r >= WINDOW) | (c >= WINDOW))
    m = lambda ok: np.where(ok, 0.0, MASKED)
    return np.concatenate([np.eye(P), m(band), m(first)], axis=1).astype(np.float32)


def sandwich_kernel(nc, x, w_hg_t, w_out_t, wqkv, wo, ln_g, ln_b, w1, b1, w2, b2,
                    tables, head_scales, consts, out):
    ctx = ExitStack()
    with ctx:
        def sb(name, shape, dt=F32):
            return ctx.enter_context(nc.sbuf_tensor(name, shape, dt))

        def sem(name):
            return ctx.enter_context(nc.semaphore(name))

        group_in = nc.dram_tensor("group_in", (LAST, 1 + GTOK, DIM), F32, kind="Internal").ap()

        def tiles_of(ap):
            return ap.rearrange("(k p) d -> p k d", p=P)

        def by_group(ap):
            return ap.rearrange("(g k p) d -> g p k d", k=GT, p=P)

        const = sb("const", [P, 3 * P])
        ident = const[:, 0:P]
        ident_bf = sb("ident_bf", [P, P], BF16)
        mask_bf = [sb(f"mask_bf{i}", [P, GT * P], BF16) for i in range(2)]
        zeros = sb("zeros", [P, P])
        w_hg_raw = sb("w_hg_raw", [P, 2 * P])
        w_hg_hi, w_hg_lo = sb("w_hg_hi", [P, 2 * P], F32R), sb("w_hg_lo", [P, 2 * P], F32R)
        w_out_sb = sb("w_out_sb", [P, P])
        wqkv_raw = [sb(f"wqkv_raw{l}", [P, 3 * INNER]) for l in range(DEPTH)]
        wqkv_hi = [sb(f"wqkv_hi{l}", [P, 3 * INNER], F32R) for l in range(DEPTH)]
        w1_raw = [sb(f"w1_raw{l}", [P, 2 * HID]) for l in range(DEPTH)]
        w1_hi = [sb(f"w1_hi{l}", [P, 2 * HID], F32R) for l in range(DEPTH)]
        wqkv_lo = [sb(f"wqkv_lo{l}", [P, 3 * INNER], F32R) for l in range(DEPTH)]
        w1_lo = [sb(f"w1_lo{l}", [P, 2 * HID], F32R) for l in range(DEPTH)]
        wo_sb = [sb(f"wo_sb{l}", [P, 4, DIM]) for l in range(DEPTH)]
        w2_sb = [sb(f"w2_sb{l}", [P, 3, DIM]) for l in range(DEPTH)]
        lngb = [sb(f"lngb{l}", [P, 2]) for l in range(DEPTH)]
        b1_sb = [sb(f"b1_sb{l}", [P, 6]) for l in range(DEPTH)]
        head_scale = sb("head_scale", [P, TABW])

        x_in = sb("x_in", [P, TILES, DIM])
        xn = sb("xn", [P, GT, DIM])
        xf_sb = sb("xf_sb", [P, GT, DIM])
        act_t_hi = sb("act_t_hi", [P, GTOK], F32R)
        act_t_lo = sb("act_t_lo", [P, GTOK], F32R)
        coef_a = sb("coef_a", [P, GTOK])
        sig_gate = sb("sig_gate", [P, GTOK])
        sig_hidden = sb("sig_hidden", [P, GTOK])
        value_b = sb("value_b", [P, GTOK])
        scan_h = sb("scan_h", [P, GTOK])
        scan_carry = sb("scan_carry", [P, 1])

        h_tok = sb("h_tok", [P, GT, DIM])
        x_res = sb("x_res", [P, GT, DIM])
        tab_raw = sb("tab_raw", [P, GT, TABW])
        tab = sb("tab", [P, GT, TABW])
        sq = sb("sq", [P, 2 * INNER])
        ss = sb("ss", [P, 2 * HEADS])
        rn = sb("rn", [P, 2 * HEADS + GT])
        nw_x, nw_t = sb("nw_x", [P, 2 * HEADS + GT]), sb("nw_t", [P, 2 * HEADS + GT])
        rot_cos = sb("rot_cos", [P, 2 * HEADS, DH])
        rot_sin = sb("rot_sin", [P, 2 * HEADS, DH])
        rot = sb("rot", [P, 2 * HEADS, DH])
        q_even = sb("q_even", [P, PAIRS, P])
        q_odd = sb("q_odd", [P, PAIRS, P])
        k_t = sb("k_t", [P, PAIRS, WINDOW + GTOK])
        v_tok = [sb(f"v_tok{i}", [P, INNER]) for i in range(GT)]
        v_mid = [sb(f"v_mid{i}", [P, INNER]) for i in range(GT)]
        neg_max = [sb(f"neg_max{i}", [P, HEADS]) for i in range(2)]
        row_sum = [sb(f"row_sum{i}", [P, HEADS]) for i in range(2)]
        inv_sum = sb("inv_sum", [P, HEADS])
        probs = sb("probs", [P, HEADS, P])
        probs_t = sb("probs_t", [P, HEADS, P])
        o_tok = sb("o_tok", [P, INNER])
        o_t = sb("o_t", [P, 4, P])
        x_attn = sb("x_attn", [P, GT + 1, DIM])
        x_early = sb("x_early", [P, 2, DIM])
        h2 = sb("h2", [P, GT, DIM])
        h2_t = sb("h2_t", [P, GTOK])
        h2_hi, h2_lo = sb("h2_hi", [P, GTOK], F32R), sb("h2_lo", [P, GTOK], F32R)
        gelu_g = sb("gelu_g", [P, 3, GTOK])
        gated = sb("gated", [P, 3, GTOK])
        y = sb("y", [P, GT, DIM])
        y_out = sb("y_out", [P, GT, DIM])
        stats = sb("stats", [P, GT, 6])
        mean_var = sb("mean_var", [P, GT, 2])
        ln_x, ln_t, ln_r = sb("ln_x", [P, GT]), sb("ln_t", [P, GT]), sb("ln_r", [P, GT])

        bank = [ctx.enter_context(nc.psum_tensor(f"bank{i}", [P, 512], F32)) for i in range(8)]
        q_bank, k_bank, v_bank = bank[0], bank[1], bank[2]
        qt_bank, kt_bank = bank[3], bank[4]
        s_bank = bank[5:7]
        misc_bank = bank[7]
        pt_bank = s_bank
        o_bank = bank[2]
        up_bank = [(bank[3], bank[4]), (bank[0], bank[1]), (bank[3], bank[4])]
        ht_bank, h2t_bank = bank[3], bank[4]
        y_bank = bank[7]

        init_done = sem("init_done")
        consts_in, w_mix_in, w_ffn_in = sem("consts_in"), sem("w_mix_in"), sem("w_ffn_in")
        x_first_in, x_rest_in = sem("x_first_in"), sem("x_rest_in")
        const_bf, w_mix_split, w_split = sem("const_bf"), sem("w_mix_split"), sem("w_split")
        zero_row, zeros_ready = sem("zero_row"), sem("zeros_ready")
        w_mix_high, w_high = sem("w_mix_high"), sem("w_high")
        xn_ready, xnt_done, xnt_hi, xnt_lo = sem("xn_ready"), sem("xnt_done"), sem("xnt_hi"), sem("xnt_lo")
        hg_done, sig_done, scan_done = sem("hg_done"), sem("sig_done"), sem("scan_done")
        mixed, mix_done, k_carried = sem("mixed"), sem("mix_done"), sem("k_carried")
        early_moved = sem("early_moved")
        xf_ready, xf_stored = sem("xf_ready"), sem("xf_stored")
        h_in, tab_in = sem("h_in"), sem("tab_in")
        res_in = [sem(f"res_in{i}") for i in range(GT)]
        v_mid_in = [sem(f"v_mid_in{i}") for i in range(GT)]
        tab_ready = sem("tab_ready")
        ht_done, ht_hi, ht_lo = sem("ht_done"), sem("ht_hi"), sem("ht_lo")
        q_done, k_done, v_done = sem("q_done"), sem("k_done"), sem("v_done")
        q_rot, k_rot, squared, rn_ready = sem("q_rot"), sem("k_rot"), sem("squared"), sem("rn_ready")
        rot_added, rot_scaled = sem("rot_added"), sem("rot_scaled")
        qt_done, kt_done, q_saved, k_saved, v_saved = sem("qt_done"), sem("kt_done"), sem("q_saved"), sem("k_saved"), sem("v_saved")
        s_done, max_ready, exp_done = sem("s_done"), sem("max_ready"), sem("exp_done")
        pt_done, pt_saved0, pt_saved1 = sem("pt_done"), sem("pt_saved0"), sem("pt_saved1")
        pv_done, o_ready, ot_done, ot_saved = sem("pv_done"), sem("o_ready"), sem("ot_done"), sem("ot_saved")
        wo_done, xa_ready = sem("wo_done"), sem("xa_ready")
        h2_in, carry_in, h2_ready = sem("h2_in"), sem("carry_in"), sem("h2_ready")
        h2t_done, h2t_saved, h2_split = sem("h2t_done"), sem("h2t_saved"), sem("h2_split")
        up_done, gelu_done, gated_done = sem("up_done"), sem("gelu_done"), sem("gated_done")
        down_done, y_read, y_ready = sem("down_done"), sem("y_read"), sem("y_ready")
        out_ready, stored = sem("out_ready"), sem("stored")
        FIRST_LAYER = 32 * GROUPS
        dve_chain = sem("dve_chain")
        settled = {e.name: sem(f"settled_{e.name}") for e in (mybir.EngineType.SP, mybir.EngineType.DVE, mybir.EngineType.Pool)}

        block = ctx.enter_context(nc.Block())

        def need(eng, s, value):
            if isinstance(value, int) and value <= 0:
                return
            eng.wait_ge(s, value)
            if eng.engine == mybir.EngineType.SP and not isinstance(value, int):
                settle(eng)

        def settle(eng):
            eng.sem_inc(settled[eng.engine.name], 1)

        class At:

            def __init__(self, G, j, back, layer):
                n = j + 2 - back
                self.t = GT * G + n
                self.slot, self.par, self.group = n % GT, n % 2, G + n // GT
                if isinstance(self.t, int):
                    self.valid = 0 <= self.t < DEPTH * TILES
                    self.layer = self.t // TILES
                    self.first = self.t % TILES == 0
                else:
                    self.valid, self.layer, self.first = True, layer, False

        def passes(eng, body, steps=None):
            body(-1, 0)
            body(0, 0)
            for layer in range(DEPTH):
                G0, G1 = GROUPS * layer + 1, GROUPS * (layer + 1) - 1
                if steps:
                    steps.enter()
                with eng.Fori(G0, G1) as G:
                    if steps:
                        steps.at(G - G0, CHAIN[layer])
                    body(G, layer)
                if steps:
                    steps.leave(G1 - G0)
                body(G1, layer)
                body(G1 + 1, layer)

        class Steps:

            def __init__(self, eng, s):
                self.eng, self.sem, self.base, self.n = eng, s, 0, 0

            def mark(self, ins):
                ins.then_inc(self.sem, 1)
                self.n += 1

            def catch_up(self):
                self.eng.wait_ge(self.sem, self.base + self.n)

            def link(self, ins):
                self.mark(ins)
                self.catch_up()

            def enter(self):
                self.start, self.n = self.base + self.n, 0

            def at(self, i, each):
                self.base, self.each = self.start + i * each, each

            def leave(self, times):
                assert self.n == self.each, f"a pass of the loop has {self.n} steps"
                self.base, self.n = self.start + times * self.each, 0

        @block.sync
        def _(sp):
            sp.dma_start(x_in[:, 0:GT, :], by_group(x)[0]).then_inc(x_first_in, 16)
            sp.dma_start(const[:, :], consts).then_inc(consts_in, 16)
            sp.dma_start(w_hg_raw[:, :], w_hg_t).then_inc(w_mix_in, 16)
            sp.dma_start(w_out_sb[:, :], w_out_t).then_inc(w_mix_in, 16)
            for g in range(1, GROUPS):
                sp.dma_start(x_in[:, GT * g:GT * g + GT, :], by_group(x)[g]).then_inc(x_rest_in, 16)
            for l in range(DEPTH):
                sp.dma_start(wqkv_raw[l][:, :], wqkv[l]).then_inc(w_ffn_in, 16)
                sp.dma_start(w1_raw[l][:, :], w1[l]).then_inc(w_ffn_in, 16)
                sp.dma_start(wo_sb[l][:, :, :], wo[l].rearrange("(c p) d -> p c d", p=P)).then_inc(w_ffn_in, 16)
                sp.dma_start(w2_sb[l][:, 0:2, :], w2[l][0:256].rearrange("(c p) d -> p c d", p=P)).then_inc(w_ffn_in, 16)
                sp.dma_start(w2_sb[l][0:TAIL, 2, :], w2[l][256:HID]).then_inc(w_ffn_in, 16)
                sp.dma_start(w2_sb[l][TAIL:TAIL + 1, 2, :], b2[l:l + 1]).then_inc(w_ffn_in, 16)
                sp.dma_start(lngb[l][:, 0:1], ln_g[l].rearrange("(p a) -> p a", a=1)).then_inc(w_ffn_in, 16)
                sp.dma_start(lngb[l][:, 1:2], ln_b[l].rearrange("(p a) -> p a", a=1)).then_inc(w_ffn_in, 16)
                for part in range(2):
                    for c, (c0, cn) in enumerate(CHUNKS):
                        src = b1[l][part * HID + c0:part * HID + c0 + cn].rearrange("(p a) -> p a", a=1)
                        sp.dma_start(b1_sb[l][0:cn, 3 * part + c:3 * part + c + 1], src).then_inc(w_ffn_in, 16)

            sp.dma_start(tab_raw[:, :, :], tables[0]).then_inc(tab_in, 16)
            sp.dma_start(head_scale[:, :], head_scales[0:1].broadcast_to([P, TABW])).then_inc(tab_in, 16)

            with sp.Fori(0, GROUPS) as g:
                need(sp, xf_ready, g + 1)
                sp.dma_start(tiles_of(group_in[g, 1:1 + GTOK, :]), xf_sb[:, :, :]).then_inc(xf_stored, 16)
                sp.dma_start(group_in[g + 1, 0:1, :], xf_sb[P - 1:P, GT - 1, :]).then_inc(xf_stored, 16)
            sp.wait_ge(xf_stored, 32 * GROUPS)
            sp.wait_ge(zeros_ready, 1)
            sp.dma_start(group_in[0, 0:1, :], zeros[0:1, :]).then_inc(zero_row, 16)
            sp.dma_start(group_in[GROUPS, 0:1, :], zeros[0:1, :]).then_inc(stored, 16)
            sp.wait_ge(zero_row, 16)
            sp.wait_ge(stored, 16)

            def load_group(G):
                need(sp, ht_done, G)
                sp.dma_start(h_tok[:, :, 0:64], tiles_of(group_in[G, 1:1 + GTOK, 0:64])).then_inc(h_in, 16)
                sp.dma_start(h_tok[:, :, 64:128], tiles_of(group_in[G, 0:GTOK, 64:128])).then_inc(h_in, 16)

            def load_tables(G):
                need(sp, tab_ready, GT * G)
                sp.dma_start(tab_raw[:, :, :], tables[G]).then_inc(tab_in, 16)
                sp.dma_start(head_scale[:, :], head_scales[G:G + 1].broadcast_to([P, TABW]) if isinstance(G, int)
                             else head_scales[bass.ds(G, 1), :].broadcast_to([P, TABW])).then_inc(tab_in, 16)

            def load_residual(G, j):
                need(sp, xa_ready, GT * (G - 1) + j + 1)
                sp.dma_start(x_res[:, j, :], group_in[G, 1 + j * P:1 + (j + 1) * P, :]).then_inc(res_in[j], 16)

            def load_h2(F):
                need(sp, xa_ready, GT * F + GT)
                need(sp, early_moved, F + 1)
                sp.dma_start(h2[0:1, :, 64:128], x_attn[P - 1:P, 0:GT, 64:128]).then_inc(h2_in, 16)
                sp.dma_start(h2[:, :, 0:64], x_attn[:, 1:GT + 1, 0:64]).then_inc(h2_in, 16)
                sp.dma_start(h2[1:113, :, 64:128], x_attn[0:112, 1:GT + 1, 64:128]).then_inc(h2_in, 16)
                sp.dma_start(h2[113:128, :, 64:128], x_attn[112:127, 1:GT + 1, 64:128]).then_inc(h2_in, 16)

            def load_carry(F):
                need(sp, h2_in, 64 * (F + 1))
                ends = isinstance(F, int) and F % GROUPS == GROUPS - 1
                last = zeros[P - 1:P, 64:128] if ends else x_attn[P - 1:P, GT, 64:128]
                sp.dma_start(x_attn[P - 1:P, 0, 64:128], last).then_inc(carry_in, 16)

            def store(F, layer):
                if layer == 0:
                    need(sp, y_ready, F + 1)
                    sp.dma_start(tiles_of(group_in[F + GROUPS, 1:1 + GTOK, :]), y[:, :, :]).then_inc(stored, 16)
                    if not (isinstance(F, int) and F == GROUPS - 1):
                        sp.dma_start(group_in[F + GROUPS + 1, 0:1, :], y[P - 1:P, GT - 1, :]).then_inc(stored, 16)
                else:
                    need(sp, out_ready, F - GROUPS + 1)
                    sp.dma_start(by_group(out)[F - GROUPS], y_out[:, :, :]).then_inc(stored, 16)
                need(sp, carry_in, 16 * (F + 1))

            load_group(0)
            for j in range(GT):
                load_residual(0, j)

            def body(G, layer):
                number = isinstance(G, int)
                for j in range(GT):
                    cur = At(G, j, 0, layer)
                    if j == 0 and not (number and not 0 <= G < LAST - 1):
                        load_tables(G + 1)
                        if layer == 0 or (number and G <= GROUPS):
                            need(sp, stored, 16 + 32 * (G - 1))
                        else:
                            sp.wait_ge(stored, FIRST_LAYER)
                        load_group(G + 1)
                    ffn = j == 1 and not (number and G < 1)
                    if ffn:
                        load_h2(G - 1)
                    if cur.valid and not (number and cur.t < GT):
                        load_residual(cur.group, cur.slot)
                    if cur.valid:
                        need(sp, pv_done, cur.t - 3)
                        need(sp, v_saved, cur.t + 1)
                        sp.dma_start(v_mid[cur.slot][0:64, :], v_tok[(cur.slot - 1) % GT][64:128, :]).then_inc(v_mid_in[cur.slot], 16)
                        sp.dma_start(v_mid[cur.slot][64:128, :], v_tok[cur.slot][0:64, :]).then_inc(v_mid_in[cur.slot], 16)
                    if ffn:
                        load_carry(G - 1)
                if not (number and G < 1):
                    store(G - 1, (G - 1) // GROUPS if number else layer)

            passes(sp, body)
            sp.wait_ge(stored, FIRST_LAYER + 16 * GROUPS)

        @block.gpsimd
        def _(pool):
            pool.memset(zeros[:, :], 0.0).then_inc(zeros_ready, 1)
            pool.memset(q_even[:, :, :], 0.0).then_inc(init_done, 1)
            pool.memset(q_odd[:, :, :], 0.0).then_inc(init_done, 1)
            pool.memset(k_t[:, :, 0:WINDOW], 0.0).then_inc(k_carried, 1)
            pool.memset(v_tok[GT - 1][:, :], 0.0).then_inc(init_done, 1)
            pool.memset(x_attn[:, 0, :], 0.0).then_inc(init_done, 1)
            pool.memset(gated[:, 2, :], 1.0).then_inc(init_done, 1)
            pool.wait_ge(w_mix_high, 1)
            pool.tensor_tensor(w_hg_lo[:, :], w_hg_raw[:, :], w_hg_hi[:, :].bitcast(F32), ALU.subtract).then_inc(w_mix_split, 1)
            for l in range(DEPTH):
                pool.wait_ge(w_high, 2 * l + 2)
                pool.tensor_tensor(wqkv_lo[l][:, :], wqkv_raw[l][:, :], wqkv_hi[l][:, :].bitcast(F32), ALU.subtract).then_inc(w_split, 1)
                pool.tensor_tensor(w1_lo[l][:, :], w1_raw[l][:, :], w1_hi[l][:, :].bitcast(F32), ALU.subtract).then_inc(w_split, 1)

            def scale_table(G, j):
                pool.wait_ge(tab_in, 32 * (G + 1))
                pool.tensor_tensor(tab[:, j, :], tab_raw[:, j, :], head_scale[:, :], ALU.mult).then_inc(tab_ready, 1)

            for j in range(GT):
                scale_table(0, j)

            def body(G, layer):
                number = isinstance(G, int)
                if number and G >= LAST:
                    return
                for j in range(GT):
                    cur = At(G, j, 0, layer)
                    if not cur.valid:
                        continue
                    t = cur.t
                    pool.wait_ge(q_rot, 2 * (t + 1))
                    pool.wait_ge(k_rot, 2 * (t + 1))
                    need(pool, kt_done, t)
                    pool.tensor_tensor(rot[:, :, 0:32], rot_cos[:, :, 0:32], rot_sin[:, :, 32:64], ALU.add).then_inc(rot_added, 1)
                    pool.tensor_tensor(rot[:, :, 32:64], rot_cos[:, :, 32:64], rot_sin[:, :, 0:32], ALU.add).then_inc(rot_added, 1)
                    if not (number and not 0 <= G < LAST - 1):
                        scale_table(G + 1, j)
                    pool.wait_ge(rn_ready, t + 1)
                    pool.wait_ge(rot_added, 2 * (t + 1))
                    pool.tensor_tensor(rot[:, :, :], rot[:, :, :],
                                       rn[:, 0:2 * HEADS].unsqueeze(2).broadcast_to([P, 2 * HEADS, DH]),
                                       ALU.mult).then_inc(rot_scaled, 1)
                    if cur.slot == 0 and not (number and G < 0):
                        pool.wait_ge(k_saved, t)
                        pool.wait_ge(s_done, 2 * (t - GT + 1))
                        settle(pool)
                        if cur.first:
                            pool.memset(k_t[:, :, 0:WINDOW], 0.0).then_inc(k_carried, 1)
                        else:
                            pool.tensor_copy(k_t[:, :, 0:WINDOW], k_t[:, :, GTOK:GTOK + WINDOW]).then_inc(k_carried, 1)
            passes(pool, body)

        W_IN = 16 * DEPTH * 14

        @block.tensor
        def _(pe):
            def product3(out_ap, lhs, rhs, lhs_lo, rhs_lo):
                pe.matmul(out_ap, lhs, rhs, start=True, stop=False)
                pe.matmul(out_ap, lhs, rhs_lo, start=False, stop=False)
                return pe.matmul(out_ap, lhs_lo, rhs, start=False, stop=True)

            def mixer(g):
                pe.wait_ge(xn_ready, g + 1)
                need(pe, xnt_lo, g)
                for k in range(GT):
                    last = pe.transpose(qt_bank[:, k * P:(k + 1) * P], xn[:, k, :], ident)
                last.then_inc(xnt_done, 1)
                pe.wait_ge(xnt_hi, g + 1)
                pe.wait_ge(xnt_lo, g + 1)
                need(pe, scan_done, g)
                for n, b in enumerate((q_bank, k_bank)):
                    cols = slice(n * P, (n + 1) * P)
                    product3(b[:, :], w_hg_hi[:, cols], act_t_hi[:, :], w_hg_lo[:, cols], act_t_lo[:, :]).then_inc(hg_done, 1)
                pe.wait_ge(scan_done, g + 1)
                need(pe, mix_done, g)
                for k in range(GT):
                    last = pe.matmul(v_bank[:, k * P:(k + 1) * P], scan_h[:, k * P:(k + 1) * P], w_out_sb[:, :],
                                     start=True, stop=True)
                last.then_inc(mixed, 1)

            pe.wait_ge(consts_in, 16)
            pe.wait_ge(w_mix_in, 32)
            pe.wait_ge(w_mix_high, 1)
            pe.wait_ge(w_mix_split, 1)
            mixer(0)
            with pe.Fori(1, GROUPS) as g:
                mixer(g)
            pe.wait_ge(mix_done, GROUPS)

            def transpose_inputs(G):
                pe.wait_ge(h_in, 32 * (G + 1))
                for k in range(GT):
                    last = pe.transpose(ht_bank[:, k * P:(k + 1) * P], h_tok[:, k, :], ident)
                last.then_inc(ht_done, 1)

            def transpose_qk(a):
                pe.wait_ge(rot_scaled, a.t + 1)
                for half, (b, ready) in enumerate(((qt_bank, qt_done), (kt_bank, kt_done))):
                    for p in range(PAIRS):
                        h = half * HEADS + 2 * p
                        last = pe.transpose(b[:, p * P:(p + 1) * P], rot[:, h:h + 2, :].rearrange("p h d -> p (h d)"), ident)
                    last.then_inc(ready, 1)

            def transpose_o(a):
                pe.wait_ge(o_ready, a.t + 1)
                need(pe, xa_ready, a.t)
                for c in range(4):
                    last = pe.transpose(misc_bank[:, c * P:(c + 1) * P], o_tok[:, c * P:(c + 1) * P], ident)
                last.then_inc(ot_done, 1)

            def project_qkv(a):
                pe.wait_ge(ht_hi, a.group + 1)
                pe.wait_ge(ht_lo, a.group + 1)
                need(pe, q_rot, 2 * a.t)
                need(pe, k_rot, 2 * a.t)
                need(pe, squared, 2 * a.t)
                tok = slice(a.slot * P, (a.slot + 1) * P)
                for n, (b, ready) in enumerate(((q_bank, q_done), (k_bank, k_done), (v_bank, v_done))):
                    w = slice(n * INNER, (n + 1) * INNER)
                    if n == 2:
                        need(pe, v_saved, a.t)
                        need(pe, o_ready, a.t - 2)
                    product3(b[:, :], act_t_hi[:, tok], wqkv_hi[a.layer][:, w],
                             act_t_lo[:, tok], wqkv_lo[a.layer][:, w]).then_inc(ready, 1)

            def transpose_probs(a, half):
                pe.wait_ge(exp_done, 2 * a.t + 1 + half)
                for h in range(4 * half, 4 * half + 4):
                    last = pe.transpose(pt_bank[half][:, (h % 4) * P:(h % 4 + 1) * P], probs[:, h, :], ident)
                last.then_inc(pt_done, 1)

            def project_out(a):
                pe.wait_ge(ot_saved, a.t + 1)
                for c in range(4):
                    last = pe.matmul(misc_bank[:, 0:DIM], o_t[:, c, :], wo_sb[a.layer][:, c, :],
                                     start=(c == 0), stop=(c == 3))
                last.then_inc(wo_done, 1)

            def scores(a, half):
                if half == 0 and a.slot == 0:
                    pe.wait_ge(k_carried, a.group + 1)
                need(pe, (pt_saved0, pt_saved1)[half], a.t)
                b = s_bank[half]
                pe.matmul(b[:, :], ident_bf[:, :], mask_bf[1 if a.first else 0][:, :], start=True, stop=True)
                for h in range(4 * half, 4 * half + 4):
                    q, col = (q_even, q_odd)[h % 2][:, h // 2, :], (h % 4) * P
                    keys = k_t[:, h // 2, a.slot * P:]
                    for low in (0, 64):
                        last = pe.matmul(b[low:low + 64, col:col + P], q[:, low:low + 64], keys[:, low:low + P],
                                         start=False, stop=True, skip_group_check=True)
                last.then_inc(s_done, 1)

            def mix_values(a):
                pe.wait_ge(pt_saved0, a.t + 1)
                pe.wait_ge(pt_saved1, a.t + 1)
                pe.wait_ge(v_mid_in[a.slot], 32 * (a.group + 1))
                need(pe, o_ready, a.t)
                pe.wait_ge(v_saved, min(a.t + 3, DEPTH * TILES) if isinstance(a.t, int) else a.t + 3)
                for h in range(HEADS):
                    cols = slice(h * DH, (h + 1) * DH)
                    for low, v in ((0, v_mid[a.slot]), (64, v_tok[a.slot])):
                        last = pe.matmul(o_bank[low:low + 64, cols], probs_t[:, h, low:low + 64], v[:, cols],
                                         start=True, stop=True)
                last.then_inc(pv_done, 1)

            def transpose_h2(F):
                pe.wait_ge(h2_ready, F + 1)
                for k in range(GT):
                    last = pe.transpose(h2t_bank[:, k * P:(k + 1) * P], h2[:, k, :], ident)
                last.then_inc(h2t_done, 1)

            def feed_forward(F, layer, t_now):
                taken = min(t_now, DEPTH * TILES) if isinstance(F, int) else t_now
                pe.wait_ge(h2_split, F + 1)
                for c, (c0, cn) in enumerate(CHUNKS):
                    if c == 1:
                        pe.wait_ge(q_rot, 2 * taken)
                        pe.wait_ge(k_rot, 2 * taken)
                        pe.wait_ge(squared, 2 * taken)
                    if c == 2:
                        pe.wait_ge(gated_done, 3 * F + 1)
                    for part, b in enumerate(up_bank[c]):
                        w = slice(part * HID + c0, part * HID + c0 + cn)
                        last = product3(b[0:cn, :], w1_hi[layer][:, w], h2_hi[:, :], w1_lo[layer][:, w], h2_lo[:, :])
                    last.then_inc(up_done, 1)
                pe.wait_ge(ot_saved, min(t_now - 3, DEPTH * TILES) if isinstance(F, int) else t_now - 3)
                pe.wait_ge(xa_ready, min(t_now - 4, DEPTH * TILES) if isinstance(F, int) else t_now - 4)
                for c, (c0, cn) in enumerate(CHUNKS):
                    pe.wait_ge(gated_done, 3 * F + c + 1)
                    for k in range(GT):
                        rows = cn + 1 if c == 2 else cn
                        last = pe.matmul(y_bank[:, k * P:(k + 1) * P], gated[0:rows, c, k * P:(k + 1) * P],
                                         w2_sb[layer][0:rows, c, :], start=(c == 0 and k == 0), stop=(c == 2),
                                         skip_group_check=True)
                last.then_inc(down_done, 1)

            pe.wait_ge(init_done, 5)
            pe.wait_ge(const_bf, 3)
            pe.wait_ge(w_ffn_in, W_IN)
            pe.wait_ge(w_high, 4)
            pe.wait_ge(w_split, 4)
            transpose_inputs(0)

            def body(G, layer):
                number = isinstance(G, int)
                for j in range(GT):
                    cur, prev, mid, done, after = (At(G, j, back, layer) for back in range(5))
                    ffn = j == 3 and not (number and G < 1)
                    if cur.valid:
                        project_qkv(cur)
                    if after.valid:
                        if j == 0 and not (number and G < 1):
                            pe.wait_ge(y_read, G)
                        project_out(after)
                    if mid.valid:
                        transpose_probs(mid, 0)
                        transpose_probs(mid, 1)
                    if prev.valid:
                        transpose_qk(prev)
                    if done.valid:
                        transpose_o(done)
                    if mid.valid:
                        mix_values(mid)
                    if prev.valid:
                        pe.wait_ge(q_saved, 2 * (prev.t + 1))
                        pe.wait_ge(k_saved, prev.t + 1)
                    if j == 1 and not (number and not 0 <= G < LAST - 1):
                        transpose_inputs(G + 1)
                    if ffn:
                        transpose_h2(G - 1)
                    if prev.valid:
                        scores(prev, 0)
                        scores(prev, 1)
                    if ffn:
                        feed_forward(G - 1, (G - 1) // GROUPS if number else layer, cur.t + 1 if not number
                                     else min(cur.t + 1, DEPTH * TILES + 4))

            passes(pe, body)

        @block.scalar
        def _(act):
            act.wait_ge(w_mix_in, 32)
            act.copy(w_hg_hi[:, :], w_hg_raw[:, :]).then_inc(w_mix_high, 1)

            def mixer(g):
                act.wait_ge(xnt_done, g + 1)
                need(act, hg_done, 2 * g)
                act.copy(act_t_hi[:, :], qt_bank[:, :]).then_inc(xnt_hi, 1)
                act.wait_ge(hg_done, 2 * g + 2)
                need(act, scan_done, g)
                act.activation(sig_hidden[:, :], q_bank[:, :], ACT.Sigmoid).then_inc(sig_done, 1)
                act.activation(sig_gate[:, :], k_bank[:, :], ACT.Sigmoid).then_inc(sig_done, 1)
                act.activation(coef_a[:, :], k_bank[:, :], ACT.Sigmoid, scale=-1.0).then_inc(sig_done, 1)

            mixer(0)
            with act.Fori(1, GROUPS) as g:
                mixer(g)
            act.wait_ge(w_ffn_in, W_IN)
            for l in range(DEPTH):
                act.copy(wqkv_hi[l][:, :], wqkv_raw[l][:, :]).then_inc(w_high, 1)
                act.copy(w1_hi[l][:, :], w1_raw[l][:, :]).then_inc(w_high, 1)
            act.wait_ge(hg_done, 2 * GROUPS)

            def save_inputs(G):
                act.wait_ge(ht_done, G + 1)
                need(act, v_done, GT * G)
                act.copy(act_t_hi[:, :], ht_bank[:, :]).then_inc(ht_hi, 1)

            save_inputs(0)

            def exponentials(a, half):
                act.wait_ge(max_ready, 2 * a.t + 1 + half)
                if half == 0:
                    need(act, pt_done, 2 * a.t)
                    need(act, o_ready, a.t - 1)
                for h in range(4 * half, 4 * half + 4):
                    last = act.activation(probs[:, h, :], s_bank[half][:, (h % 4) * P:(h % 4 + 1) * P], ACT.Exp,
                                          bias=neg_max[a.par][:, h:h + 1], accum_out=row_sum[a.par][:, h:h + 1])
                last.then_inc(exp_done, 1)

            def body(G, layer):
                number = isinstance(G, int)
                for j in range(GT):
                    cur, prev, mid, done = (At(G, j, back, layer) for back in range(4))
                    if mid.valid:
                        exponentials(mid, 0)
                        exponentials(mid, 1)
                    if cur.valid:
                        act.wait_ge(v_done, cur.t + 1)
                        need(act, pv_done, cur.t - 3)
                        if not (number and cur.t < GT):
                            moved = At(G, j, 3, layer)
                            act.wait_ge(v_mid_in[moved.slot], 32 * (moved.group + 1))
                        act.copy(v_tok[cur.slot][:, :], v_bank[:, :]).then_inc(v_saved, 1)
                        need(act, rn_ready, cur.t)
                        for n, (b, read) in enumerate(((q_bank, q_rot), (k_bank, k_rot))):
                            act.wait_ge(read, 2 * (cur.t + 1))
                            act.activation(sq[:, n * INNER:(n + 1) * INNER], b[:, :], ACT.Square).then_inc(squared, 1)
                    if mid.valid:
                        act.wait_ge(pt_done, 2 * mid.t + 1)
                        need(act, pv_done, mid.t)
                        act.copy(probs_t[:, 0:4, :], pt_bank[0][:, :].rearrange("p (h t) -> p h t", h=4)).then_inc(pt_saved0, 1)
                    if prev.valid:
                        act.wait_ge(qt_done, prev.t + 1)
                        need(act, s_done, 2 * prev.t)
                        act.copy(q_even[0:64, :, :], qt_bank[0:64, :].rearrange("p (c t) -> p c t", c=PAIRS)).then_inc(q_saved, 1)
                        act.copy(q_odd[64:128, :, :], qt_bank[64:128, :].rearrange("p (c t) -> p c t", c=PAIRS)).then_inc(q_saved, 1)
                        act.wait_ge(kt_done, prev.t + 1)
                        if prev.slot == GT - 1:
                            act.wait_ge(k_carried, prev.group + 1)
                        act.copy(k_t[:, :, WINDOW + prev.slot * P:WINDOW + (prev.slot + 1) * P],
                                 kt_bank[:, :].rearrange("p (c t) -> p c t", c=PAIRS)).then_inc(k_saved, 1)
                    if done.valid:
                        act.wait_ge(ot_done, done.t + 1)
                        need(act, wo_done, done.t)
                        act.copy(o_t[:, :, :], misc_bank[:, :].rearrange("p (c t) -> p c t", c=4)).then_inc(ot_saved, 1)
                    if j == 1 and not (number and not 0 <= G < LAST - 1):
                        save_inputs(G + 1)
                    if j == 3 and not (number and G < 1):
                        F = G - 1
                        l = F // GROUPS if number else layer
                        act.wait_ge(h2t_done, F + 1)
                        for dst in (h2_hi, h2_t):
                            act.activation(dst[:, :], h2t_bank[:, :], ACT.Identity, bias=lngb[l][:, 1:2],
                                           scale=lngb[l][:, 0:1]).then_inc(h2t_saved, 1)
                        for c, (c0, cn) in enumerate(CHUNKS):
                            act.wait_ge(up_done, 3 * F + c + 1)
                            act.activation(gelu_g[0:cn, c, :], up_bank[c][1][0:cn, :], ACT.Gelu,
                                           bias=b1_sb[l][0:cn, 3 + c:4 + c]).then_inc(gelu_done, 1)

            passes(act, body)

        @block.vector
        def _(dve):
            steps = Steps(dve, dve_chain)
            link = steps.link

            def rsqrt(out_ap, x_ap, half_ap, tmp):
                link(dve.tensor_scalar(out_ap.bitcast(I32), x_ap.bitcast(I32), -0.5, float(RSQRT_SEED), ALU.mult, ALU.add))
                link(dve.tensor_scalar(half_ap, x_ap, -0.5, None, ALU.mult))
                for n in range(3):
                    link(dve.tensor_tensor(tmp, out_ap, out_ap, ALU.mult))
                    link(dve.tensor_tensor(tmp, tmp, half_ap, ALU.mult))
                    last = dve.scalar_tensor_tensor(out_ap, tmp, 1.5, out_ap, ALU.add, ALU.mult)
                    if n < 2:
                        link(last)
                return last

            def moments(src):
                settle(dve)
                for k in range(GT):
                    last = dve.bn_stats(stats[:, k, :], src(k))
                link(last)
                settle(dve)
                for k in range(GT):
                    last = dve.bn_aggr(mean_var[:, k, :], stats[:, k, :])
                link(last)
                link(dve.tensor_scalar(ln_x[:, :], mean_var[:, :, 1], LN_EPS, None, ALU.add))
                link(rsqrt(ln_r[:, :], ln_x[:, :], ln_x[:, :], ln_t[:, :]))

            def normalise(dst, src):
                for k in range(GT):
                    last = dve.tensor_scalar(dst(k), src(k), mean_var[:, k, 0:1], ln_r[:, k:k + 1], ALU.subtract, ALU.mult)
                return last

            dve.wait_ge(consts_in, 16)
            dve.tensor_copy(ident_bf[:, :], ident).then_inc(const_bf, 1)
            for n, m in enumerate(mask_bf):
                src = const[:, (n + 1) * P:(n + 2) * P]
                dve.tensor_copy(m[:, :].rearrange("p (h k) -> p h k", h=GT),
                                src.unsqueeze(1).broadcast_to([P, GT, P])).then_inc(const_bf, 1)

            def mixer(g, carry):
                tile = lambda k: x_in[:, GT * g + k, :]
                moments(tile)
                need(dve, xnt_done, g)
                normalise(lambda k: xn[:, k, :], tile).then_inc(xn_ready, 1)
                dve.wait_ge(xnt_hi, g + 1)
                dve.tensor_tensor(act_t_lo[:, :], qt_bank[:, :], act_t_hi[:, :].bitcast(F32), ALU.subtract).then_inc(xnt_lo, 1)
                dve.wait_ge(sig_done, 3 * g + 3)
                link(dve.tensor_scalar(sig_hidden[:, :], sig_hidden[:, :], 0.5, None, ALU.min))
                link(dve.scalar_tensor_tensor(value_b[:, :], q_bank[:, :], 0.0, sig_hidden[:, :], ALU.max, ALU.add))
                link(dve.tensor_tensor(value_b[:, :], value_b[:, :], sig_gate[:, :], ALU.mult))
                need(dve, mixed, g)
                dve.tensor_tensor_scan(scan_h[:, :], coef_a[:, :], value_b[:, :], scan_carry[:, 0:1] if carry else 0.0,
                                       ALU.mult, ALU.add).then_inc(scan_done, 1)
                dve.wait_ge(scan_done, g + 1)
                dve.tensor_copy(scan_carry[:, :], scan_h[:, GTOK - 1:GTOK])
                dve.wait_ge(mixed, g + 1)
                out_k = lambda k: v_bank[:, k * P:(k + 1) * P]
                moments(out_k)
                last = normalise(lambda k: y[:, k, :], out_k)
                last.then_inc(mix_done, 1)
                dve.wait_ge(mix_done, g + 1)
                group = x_in[:, bass.ds(GT * g, GT), :] if not isinstance(g, int) else x_in[:, GT * g:GT * g + GT, :]
                link(dve.tensor_tensor(group, group, y[:, :, :], ALU.add))
                moments(tile)
                need(dve, xf_stored, 32 * g)
                normalise(lambda k: xf_sb[:, k, :], tile).then_inc(xf_ready, 1)

            dve.wait_ge(x_first_in, 16)
            mixer(0, False)
            dve.wait_ge(x_rest_in, 16 * (GROUPS - 1))
            steps.enter()
            with dve.Fori(1, GROUPS) as g:
                steps.at(g - 1, CHAIN["mix"])
                mixer(g, True)
            steps.leave(GROUPS - 1)

            def split_inputs(G):
                dve.wait_ge(ht_hi, G + 1)
                need(dve, v_done, GT * G)
                dve.tensor_tensor(act_t_lo[:, :], ht_bank[:, :], act_t_hi[:, :].bitcast(F32), ALU.subtract).then_inc(ht_lo, 1)

            split_inputs(0)

            def rotate(a):
                dve.wait_ge(tab_ready, a.t + 1)
                need(dve, rot_added, 2 * a.t)
                for n, (b, ready, done) in enumerate(((q_bank, q_done, q_rot), (k_bank, k_done, k_rot))):
                    dve.wait_ge(ready, a.t + 1)
                    src = b[:, :].rearrange("p (h d) -> p h d", h=HEADS)
                    for m, dst in enumerate((rot_cos, rot_sin)):
                        table = tab[:, a.slot, (2 * n + m) * DH:(2 * n + m + 1) * DH]
                        dve.tensor_tensor(dst[:, n * HEADS:(n + 1) * HEADS, :], src,
                                          table.unsqueeze(1).broadcast_to([P, HEADS, DH]), ALU.mult).then_inc(done, 1)

            def sum_squares(a):
                dve.wait_ge(squared, 2 * (a.t + 1))
                link(dve.tensor_reduce(ss[:, :], sq[:, :].rearrange("p (h d) -> p h d", h=2 * HEADS), AX.X, ALU.add))
                steps.mark(dve.tensor_scalar(nw_x[:, 0:2 * HEADS], ss[:, :], NORM_FLOOR, -0.5, ALU.max, ALU.mult))

            def variances_h2(F):
                dve.wait_ge(h2_in, 64 * (F + 1))
                settle(dve)
                for k in range(GT):
                    last = dve.bn_stats(stats[:, k, :], h2[:, k, :])
                link(last)
                settle(dve)
                for k in range(GT):
                    last = dve.bn_aggr(mean_var[:, k, :], stats[:, k, :])
                link(last)
                steps.mark(dve.tensor_scalar(nw_x[:, 2 * HEADS:], mean_var[:, :, 1], LN_EPS, -0.5, ALU.add, ALU.mult))

            def newton_seed(cols):
                steps.catch_up()
                steps.mark(dve.tensor_scalar(rn[:, cols].bitcast(I32), nw_x[:, cols].bitcast(I32), -0.5,
                                               float(RSQRT_SEED - 2 ** 30 - 2 ** 22), ALU.mult, ALU.add))

            def newton_round(cols):
                steps.catch_up()
                link(dve.tensor_tensor(nw_t[:, cols], rn[:, cols], rn[:, cols], ALU.mult))
                link(dve.tensor_tensor(nw_t[:, cols], nw_t[:, cols], nw_x[:, cols], ALU.mult))
                return dve.scalar_tensor_tensor(rn[:, cols], nw_t[:, cols], 1.5, rn[:, cols], ALU.add, ALU.mult)

            def normalise_h2(F):
                steps.catch_up()
                for k in range(GT):
                    col = 2 * HEADS + k
                    last = dve.tensor_scalar(h2[:, k, :], h2[:, k, :], mean_var[:, k, 0:1], rn[:, col:col + 1],
                                             ALU.subtract, ALU.mult)
                last.then_inc(h2_ready, 1)

            def save_probs(a):
                dve.wait_ge(pt_done, 2 * a.t + 2)
                need(dve, pv_done, a.t)
                dve.tensor_copy(probs_t[:, 4:8, :], pt_bank[1][:, :].rearrange("p (h t) -> p h t", h=4)).then_inc(pt_saved1, 1)

            def add_residual(a):
                dve.wait_ge(wo_done, a.t + 1)
                dve.wait_ge(res_in[a.slot], 16 * (a.group + 1))
                dst = x_early[:, a.slot, :] if a.slot < 2 else x_attn[:, a.slot + 1, :]
                dve.tensor_tensor(dst, misc_bank[:, 0:DIM], x_res[:, a.slot, :], ALU.add).then_inc(xa_ready, 1)

            def row_max(a, half):
                dve.wait_ge(s_done, 2 * a.t + 1 + half)
                need(dve, exp_done, 2 * (a.t - 1))
                src = s_bank[half][:, :].rearrange("p (h k) -> p h k", h=4)
                dve.tensor_reduce(neg_max[a.par][:, 4 * half:4 * half + 4], src, AX.X, ALU.max, negate=True).then_inc(max_ready, 1)

            def divide_o(a):
                dve.wait_ge(exp_done, 2 * a.t + 2)
                link(dve.reciprocal(inv_sum[:, :], row_sum[a.par][:, :]))
                dve.wait_ge(pv_done, a.t + 1)
                need(dve, ot_done, a.t)
                dve.tensor_tensor(o_tok[:, :].rearrange("p (h d) -> p h d", h=HEADS),
                                  o_bank[:, :].rearrange("p (h d) -> p h d", h=HEADS),
                                  inv_sum[:, :].unsqueeze(2).broadcast_to([P, HEADS, DH]), ALU.mult).then_inc(o_ready, 1)

            def split_h2(F):
                dve.wait_ge(h2t_saved, 2 * (F + 1))
                dve.tensor_tensor(h2_lo[:, :], h2_t[:, :], h2_hi[:, :].bitcast(F32), ALU.subtract).then_inc(h2_split, 1)

            def gate(F, layer, c, cn):
                dve.wait_ge(gelu_done, 3 * F + c + 1)
                dve.scalar_tensor_tensor(gated[0:cn, c, :], up_bank[c][0][0:cn, :], b1_sb[layer][0:cn, c:c + 1],
                                         gelu_g[0:cn, c, :], ALU.add, ALU.mult).then_inc(gated_done, 1)

            def place_early(G):
                if not (isinstance(G, int) and G >= LAST):
                    dve.wait_ge(xa_ready, GT * G + 2)
                    dve.tensor_copy(x_attn[:, 1:3, :], x_early[:, :, :]).then_inc(early_moved, 1)

            def finish_group(F, layer):
                dve.wait_ge(down_done, F + 1)
                dve.wait_ge(stored, 16 + 32 * F if layer == 0 else FIRST_LAYER)
                add = dve.tensor_tensor(y[:, :, :], y_bank[:, :].rearrange("p (k d) -> p k d", k=GT),
                                        x_attn[:, 1:GT + 1, :], ALU.add)
                add.then_inc(y_read, 1)
                dve.wait_ge(y_read, F + 2)
                dve.wait_ge(carry_in, 16 * (F + 1))
                place_early(F + 1)
                if layer == 0:
                    dve.nop().then_inc(y_ready, 1)
                else:
                    g = F - GROUPS
                    tile = lambda k: y[:, k, :]
                    moments(tile)
                    dve.wait_ge(stored, FIRST_LAYER + 16 * g)
                    link(normalise(lambda k: y_out[:, k, :], tile))
                    group = x_in[:, GT * g:GT * g + GT, :] if isinstance(g, int) else x_in[:, bass.ds(GT * g, GT), :]
                    dve.tensor_tensor(y_out[:, :, :], y_out[:, :, :], group, ALU.add).then_inc(out_ready, 1)

            def body(G, layer):
                number = isinstance(G, int)
                for j in range(GT):
                    cur, mid, done, after = (At(G, j, back, layer) for back in (0, 2, 3, 4))
                    norm, ffn = (j == n and not (number and G < 1) for n in (2, 3))
                    if mid.valid:
                        row_max(mid, 0)
                    if done.valid:
                        divide_o(done)
                    if mid.valid:
                        row_max(mid, 1)
                    if cur.valid:
                        rotate(cur)
                    if after.valid:
                        add_residual(after)
                    if mid.valid:
                        save_probs(mid)
                    if cur.valid:
                        sum_squares(cur)
                    if norm:
                        variances_h2(G - 1)
                    if ffn:
                        dve.wait_ge(rn_ready, min(cur.t, DEPTH * TILES) if number else cur.t)
                        normalise_h2(G - 1)
                    if cur.valid or norm:
                        cols = slice(0 if cur.valid else 2 * HEADS, 2 * HEADS + (GT if norm else 0))
                        if cur.valid:
                            need(dve, rot_scaled, cur.t)
                        elif norm:
                            dve.wait_ge(rot_scaled, DEPTH * TILES)
                        newton_seed(cols)
                        steps.mark(newton_round(cols))
                        steps.mark(newton_round(cols))
                        last = newton_round(cols)
                        if cur.valid:
                            last.then_inc(rn_ready, 1)
                        else:
                            steps.mark(last)
                    if j == 1 and not (number and not 0 <= G < LAST - 1):
                        split_inputs(G + 1)
                    if ffn:
                        split_h2(G - 1)
                        l = (G - 1) // GROUPS if number else layer
                        for c, (c0, cn) in enumerate(CHUNKS):
                            gate(G - 1, l, c, cn)
                        finish_group(G - 1, l)
                    elif j == 3 and number and G == 0:
                        dve.nop().then_inc(y_read, 1)
                        place_early(0)

            passes(dve, body, steps)


def kernel(L0_attn_x, L0_attn_W_hg, L0_attn_W_out, L0_ffn_wqkv, L0_ffn_q_scale, L0_ffn_k_scale, L0_ffn_wo,
           L0_ffn_ln_g, L0_ffn_ln_b, L0_ffn_w1, L0_ffn_b1, L0_ffn_w2, L0_ffn_b2):
    import concourse.bacc as bacc
    from concourse.bass_utils import run_bass_kernel_spmd

    tables = np.tile(rotary_tables().reshape(GROUPS, GT, P, TABW).transpose(0, 2, 1, 3), (DEPTH, 1, 1, 1))
    q_s, k_s = np.asarray(L0_ffn_q_scale), np.asarray(L0_ffn_k_scale)
    head_scales = np.repeat(np.concatenate([q_s, q_s, k_s, k_s], axis=1), GROUPS, axis=0)
    arrays = {
        "x": np.asarray(L0_attn_x).reshape(N, DIM),
        "w_hg_t": np.asarray(L0_attn_W_hg).T,
        "w_out_t": np.asarray(L0_attn_W_out).T,
        "wqkv": L0_ffn_wqkv, "wo": L0_ffn_wo,
        "ln_g": L0_ffn_ln_g, "ln_b": L0_ffn_ln_b, "w1": L0_ffn_w1, "b1": L0_ffn_b1, "w2": L0_ffn_w2,
        "b2": L0_ffn_b2, "tables": tables, "head_scales": head_scales, "consts": constant_block(),
    }
    arrays = {k: np.ascontiguousarray(v) for k, v in arrays.items()}
    nc = bacc.Bacc("TRN2", target_bir_lowering=False, num_devices=1)
    args = [nc.dram_tensor(k, a.shape, mybir.dt.from_np(a.dtype), kind="ExternalInput").ap() for k, a in arrays.items()]
    out = nc.dram_tensor("out", (N, DIM), F32, kind="ExternalOutput").ap()
    sandwich_kernel(nc, *args, out)
    r = run_bass_kernel_spmd(nc, [arrays], core_ids=[0])
    return r.results[0]["out"].reshape(1, N, DIM)
```

```python
from contextlib import ExitStack

import numpy as np

import concourse.bass as bass
from concourse import mybir

F32 = mybir.dt.float32
F32R = mybir.dt.float32r
BF16 = mybir.dt.bfloat16
I32 = mybir.dt.int32
ALU = mybir.AluOpType
ACT = mybir.ActivationFunctionType
AX = mybir.AxisListType

P = 128
DIM = 128
N = 2048
HEADS, DH, WINDOW = 8, 64, 64
INNER = HEADS * DH
PAIRS = HEADS // 2
HID = int(DIM * 4 * 2 / 3)
DEPTH = 2
TILES = N // P
GT = 4
GROUPS = TILES // GT
GTOK = GT * P
LAST = DEPTH * GROUPS
CHUNKS = [(0, 128), (128, 128), (256, HID - 256)]
TAIL = HID - 256
TABW = 4 * DH
MASKED = -1.0e30
LN_EPS = 1e-5
NORM_FLOOR = 1e-24
RSQRT_SEED = 0x5F3759DF

CHAIN = {0: 43, 1: 46}


def rotary_tables():
    half = np.arange(0, DH, 2, dtype=np.float32)
    inv = (np.float32(1.0) / np.power(np.float32(10000.0), half / np.float32(DH))).astype(np.float32)
    t = np.arange(N, dtype=np.float32)
    freqs = (t[:, None] * inv[None, :]).astype(np.float32).astype(np.float64)
    base = ((half + np.float32(0.4 * DH)) / np.float32(1.4 * DH)).astype(np.float32).astype(np.float64)
    power = (t.astype(np.float64) - N // 2) / float(WINDOW // 2)
    scale = base[None, :] ** power[:, None]
    cos, sin = np.cos(freqs), np.sin(freqs)
    both = lambda a, b: np.concatenate([a, b], axis=1)
    q, k = 8.0 * scale, 1.0 / scale
    return np.concatenate([both(cos * q, cos * q), both(sin * q, -sin * q),
                           both(cos * k, cos * k), both(sin * k, -sin * k)], axis=1).astype(np.float32)


def constant_block():
    r, c = np.arange(P)[:, None], np.arange(P)[None, :]
    a = r % WINDOW
    band = (c >= a) & (c <= a + WINDOW)
    first = band & ((r >= WINDOW) | (c >= WINDOW))
    m = lambda ok: np.where(ok, 0.0, MASKED)
    return np.concatenate([np.eye(P), m(band), m(first)], axis=1).astype(np.float32)


def sandwich_kernel(nc, x, w_hg_t, w_out_t, wqkv, wo, ln_g, ln_b, w1, b1, w2, b2,
                    tables, head_scales, consts, out):
    ctx = ExitStack()
    with ctx:
        def sb(name, shape, dt=F32):
            return ctx.enter_context(nc.sbuf_tensor(name, shape, dt))

        def sem(name):
            return ctx.enter_context(nc.semaphore(name))

        group_in = nc.dram_tensor("group_in", (LAST, 1 + GTOK, DIM), F32, kind="Internal").ap()

        def tiles_of(ap):
            return ap.rearrange("(k p) d -> p k d", p=P)

        def group_tiles(ap, g):
            return ap[:, GT * g:GT * g + GT, :] if isinstance(g, int) else ap[:, bass.ds(GT * g, GT), :]

        def by_group(ap):
            return ap.rearrange("(g k p) d -> g p k d", k=GT, p=P)

        const = sb("const", [P, 3 * P])
        ident = const[:, 0:P]
        ident_bf = sb("ident_bf", [P, P], BF16)
        mask_bf = [sb(f"mask_bf{i}", [P, GT * P], BF16) for i in range(2)]
        zeros = sb("zeros", [P, P])
        w_hg_raw = sb("w_hg_raw", [P, 2 * P])
        w_hg_hi, w_hg_lo = sb("w_hg_hi", [P, 2 * P], F32R), sb("w_hg_lo", [P, 2 * P], F32R)
        w_out_sb = sb("w_out_sb", [P, P])
        wqkv_raw = [sb(f"wqkv_raw{l}", [P, 3 * INNER]) for l in range(DEPTH)]
        wqkv_hi = [sb(f"wqkv_hi{l}", [P, 3 * INNER], F32R) for l in range(DEPTH)]
        w1_raw = [sb(f"w1_raw{l}", [P, 2 * HID]) for l in range(DEPTH)]
        w1_hi = [sb(f"w1_hi{l}", [P, 2 * HID], F32R) for l in range(DEPTH)]
        wqkv_lo = [sb(f"wqkv_lo{l}", [P, 3 * INNER], F32R) for l in range(DEPTH)]
        w1_lo = [sb(f"w1_lo{l}", [P, 2 * HID], F32R) for l in range(DEPTH)]
        wo_sb = [sb(f"wo_sb{l}", [P, 4, DIM]) for l in range(DEPTH)]
        w2_sb = [sb(f"w2_sb{l}", [P, 3, DIM]) for l in range(DEPTH)]
        lngb = [sb(f"lngb{l}", [P, 2]) for l in range(DEPTH)]
        b1_sb = [sb(f"b1_sb{l}", [P, 6]) for l in range(DEPTH)]
        head_scale = sb("head_scale", [P, TABW])

        x_in = sb("x_in", [P, TILES, DIM])
        normed = sb("normed", [P, TILES, DIM])
        act_t_hi = sb("act_t_hi", [P, GTOK], F32R)
        act_t_lo = sb("act_t_lo", [P, GTOK], F32R)
        coef_a = sb("coef_a", [P, GTOK])
        sig_gate = sb("sig_gate", [P, GTOK])
        sig_hidden = sb("sig_hidden", [P, GTOK])
        value_b = sb("value_b", [P, GTOK])
        scan_h = sb("scan_h", [P, GTOK])
        scan_carry = sb("scan_carry", [P, 1])

        h_tok = sb("h_tok", [P, GT, DIM])
        x_res = sb("x_res", [P, GT, DIM])
        tab_raw = sb("tab_raw", [P, GT, TABW])
        tab = sb("tab", [P, GT, TABW])
        sq = sb("sq", [P, 2 * INNER])
        ss = sb("ss", [P, 2 * HEADS])
        rn = sb("rn", [P, 2 * HEADS + GT])
        nw_x, nw_t = sb("nw_x", [P, 2 * HEADS + GT]), sb("nw_t", [P, 2 * HEADS + GT])
        rot_cos = sb("rot_cos", [P, 2 * HEADS, DH])
        rot_sin = sb("rot_sin", [P, 2 * HEADS, DH])
        rot = sb("rot", [P, 2 * HEADS, DH])
        q_even = sb("q_even", [P, PAIRS, P])
        q_odd = sb("q_odd", [P, PAIRS, P])
        k_t = sb("k_t", [P, PAIRS, WINDOW + GTOK])
        v_tok = [sb(f"v_tok{i}", [P, INNER]) for i in range(GT)]
        v_mid = [sb(f"v_mid{i}", [P, INNER]) for i in range(GT)]
        neg_max = [sb(f"neg_max{i}", [P, HEADS]) for i in range(2)]
        row_sum = [sb(f"row_sum{i}", [P, HEADS]) for i in range(2)]
        inv_sum = sb("inv_sum", [P, HEADS])
        probs = sb("probs", [P, HEADS, P])
        probs_t = sb("probs_t", [P, HEADS, P])
        o_tok = sb("o_tok", [P, INNER])
        o_t = sb("o_t", [P, 4, P])
        x_attn = sb("x_attn", [P, GT + 1, DIM])
        x_early = sb("x_early", [P, 2, DIM])
        h2 = sb("h2", [P, GT, DIM])
        h2_t = sb("h2_t", [P, GTOK])
        h2_hi, h2_lo = sb("h2_hi", [P, GTOK], F32R), sb("h2_lo", [P, GTOK], F32R)
        gelu_g = sb("gelu_g", [P, 3, GTOK])
        gated = sb("gated", [P, 3, GTOK])
        y = sb("y", [P, GT, DIM])
        y_out = sb("y_out", [P, GT, DIM])
        stats = sb("stats", [P, TILES + GT, 6])
        mean_var = sb("mean_var", [P, TILES + GT, 2])
        shift = sb("shift", [P, TILES])

        bank = [ctx.enter_context(nc.psum_tensor(f"bank{i}", [P, 512], F32)) for i in range(4)]
        upper = ctx.enter_context(nc.psum_tensor("upper", [P, 4, 512], F32))
        bank += [upper[:, i, :] for i in range(4)]
        mix_out = upper
        q_bank, k_bank, v_bank = bank[0], bank[1], bank[2]
        qt_bank, kt_bank = bank[3], bank[4]
        s_bank = bank[5:7]
        misc_bank = bank[7]
        pt_bank = s_bank
        o_bank = bank[2]
        up_bank = [(bank[3], bank[4]), (bank[0], bank[1]), (bank[7], bank[2])]
        ht_bank, h2t_bank = bank[3], bank[4]
        y_bank = bank[3]

        init_done = sem("init_done")
        consts_in, w_mix_in, w_ffn_in = sem("consts_in"), sem("w_mix_in"), sem("w_ffn_in")
        x_in_done = [sem(f"x_in_done{g}") for g in range(GROUPS)]
        w_big_in, hidden_read, x1_ready = sem("w_big_in"), sem("hidden_read"), sem("x1_ready")
        const_bf, w_mix_split, w_split = sem("const_bf"), sem("w_mix_split"), sem("w_split")
        zero_row, zeros_ready = sem("zero_row"), sem("zeros_ready")
        w_mix_high, w_high = sem("w_mix_high"), sem("w_high")
        xn_ready, xnt_done, xnt_hi, xnt_lo = sem("xn_ready"), sem("xnt_done"), sem("xnt_hi"), sem("xnt_lo")
        hg_done, sig_done, scan_done = sem("hg_done"), sem("sig_done"), sem("scan_done")
        mixed, mix_done, k_carried = sem("mixed"), sem("mix_done"), sem("k_carried")
        mix_act, shift_ready = sem("mix_act"), sem("shift_ready")
        early_moved = sem("early_moved")
        xf_ready, xf_stored = sem("xf_ready"), sem("xf_stored")
        h_in, tab_in = sem("h_in"), sem("tab_in")
        h_first_in, x_res_first = sem("h_first_in"), sem("x_res_first")
        res_in = [sem(f"res_in{i}") for i in range(GT)]
        v_mid_in = [sem(f"v_mid_in{i}") for i in range(GT)]
        tab_ready = sem("tab_ready")
        ht_done, ht_hi, ht_lo = sem("ht_done"), sem("ht_hi"), sem("ht_lo")
        q_done, k_done, v_done = sem("q_done"), sem("k_done"), sem("v_done")
        q_rot, k_rot, squared, rn_ready = sem("q_rot"), sem("k_rot"), sem("squared"), sem("rn_ready")
        rot_added, rot_scaled = sem("rot_added"), sem("rot_scaled")
        qt_done, kt_done, q_saved, k_saved, v_saved = sem("qt_done"), sem("kt_done"), sem("q_saved"), sem("k_saved"), sem("v_saved")
        s_done, max_ready, exp_done = sem("s_done"), sem("max_ready"), sem("exp_done")
        pt_done, pt_saved0, pt_saved1 = sem("pt_done"), sem("pt_saved0"), sem("pt_saved1")
        pv_done, o_ready, ot_done, ot_saved = sem("pv_done"), sem("o_ready"), sem("ot_done"), sem("ot_saved")
        wo_done, xa_ready = sem("wo_done"), sem("xa_ready")
        h2_in, carry_in, h2_ready = sem("h2_in"), sem("carry_in"), sem("h2_ready")
        h2t_done, h2t_saved, h2_split = sem("h2t_done"), sem("h2t_saved"), sem("h2_split")
        up_done, gelu_done, gated_done = sem("up_done"), sem("gelu_done"), sem("gated_done")
        down_done, y_read, y_ready = sem("down_done"), sem("y_read"), sem("y_ready")
        out_ready, stored = sem("out_ready"), sem("stored")
        FIRST_LAYER = 32 * GROUPS
        y_normed = sem("y_normed")
        dve_chain = sem("dve_chain")
        settled = {e.name: sem(f"settled_{e.name}") for e in (mybir.EngineType.SP, mybir.EngineType.DVE, mybir.EngineType.Pool)}

        block = ctx.enter_context(nc.Block())

        def need(eng, s, value):
            if isinstance(value, int) and value <= 0:
                return
            eng.wait_ge(s, value)
            if eng.engine == mybir.EngineType.SP and not isinstance(value, int):
                settle(eng)

        def settle(eng):
            eng.sem_inc(settled[eng.engine.name], 1)

        class At:

            def __init__(self, G, j, back, layer):
                n = j + 3 - back
                self.t = GT * G + n
                self.slot, self.par, self.group = n % GT, n % 2, G + n // GT
                if isinstance(self.t, int):
                    self.valid = 0 <= self.t < DEPTH * TILES
                    self.layer = self.t // TILES
                    self.first = self.t % TILES == 0
                else:
                    self.valid, self.layer, self.first = True, layer, False

        def passes(eng, body, steps=None):
            body(-1, 0)
            body(0, 0)
            for layer in range(DEPTH):
                G0, G1 = GROUPS * layer + 1, GROUPS * (layer + 1) - 1
                if steps:
                    steps.enter()
                with eng.Fori(G0, G1) as G:
                    if steps:
                        steps.at(G - G0, CHAIN[layer])
                    body(G, layer)
                if steps:
                    steps.leave(G1 - G0)
                body(G1, layer)
                body(G1 + 1, layer)

        class Steps:

            def __init__(self, eng, s):
                self.eng, self.sem, self.base, self.n = eng, s, 0, 0

            def mark(self, ins):
                ins.then_inc(self.sem, 1)
                self.n += 1

            def catch_up(self):
                self.eng.wait_ge(self.sem, self.base + self.n)

            def link(self, ins):
                self.mark(ins)
                self.catch_up()

            def enter(self):
                self.start, self.n = self.base + self.n, 0

            def at(self, i, each):
                self.base, self.each = self.start + i * each, each

            def leave(self, times):
                assert self.n == self.each, f"a pass of the loop has {self.n} steps"
                self.base, self.n = self.start + times * self.each, 0

        @block.sync
        def _(sp):
            for g in range(GROUPS):
                sp.dma_start(x_in[:, GT * g:GT * g + GT, :], by_group(x)[g]).then_inc(x_in_done[g], 16)
            sp.dma_start(const[:, :], consts).then_inc(consts_in, 16)
            sp.dma_start(w_hg_raw[:, :], w_hg_t).then_inc(w_mix_in, 16)
            sp.dma_start(w_out_sb[:, :], w_out_t).then_inc(w_mix_in, 16)
            for l in range(DEPTH):
                sp.dma_start(wqkv_raw[l][:, :], wqkv[l]).then_inc(w_big_in, 16)
                sp.dma_start(w1_raw[l][:, :], w1[l]).then_inc(w_big_in, 16)
            sp.dma_start(tab_raw[:, :, :], tables[0]).then_inc(tab_in, 16)
            sp.dma_start(head_scale[:, :], head_scales[0:1].broadcast_to([P, TABW])).then_inc(tab_in, 16)
            for l in range(DEPTH):
                sp.dma_start(wo_sb[l][:, :, :], wo[l].rearrange("(c p) d -> p c d", p=P)).then_inc(w_ffn_in, 16)
                sp.dma_start(w2_sb[l][:, 0:2, :], w2[l][0:256].rearrange("(c p) d -> p c d", p=P)).then_inc(w_ffn_in, 16)
                sp.dma_start(w2_sb[l][0:TAIL, 2, :], w2[l][256:HID]).then_inc(w_ffn_in, 16)
                sp.dma_start(w2_sb[l][TAIL:TAIL + 1, 2, :], b2[l:l + 1]).then_inc(w_ffn_in, 16)
                sp.dma_start(lngb[l][:, 0:1], ln_g[l].rearrange("(p a) -> p a", a=1)).then_inc(w_ffn_in, 16)
                sp.dma_start(lngb[l][:, 1:2], ln_b[l].rearrange("(p a) -> p a", a=1)).then_inc(w_ffn_in, 16)
                for part in range(2):
                    for c, (c0, cn) in enumerate(CHUNKS):
                        src = b1[l][part * HID + c0:part * HID + c0 + cn].rearrange("(p a) -> p a", a=1)
                        sp.dma_start(b1_sb[l][0:cn, 3 * part + c:3 * part + c + 1], src).then_inc(w_ffn_in, 16)
            sp.wait_ge(zeros_ready, 1)
            sp.dma_start(group_in[0, 0:1, :], zeros[0:1, :]).then_inc(zero_row, 16)
            sp.dma_start(group_in[GROUPS, 0:1, :], zeros[0:1, :]).then_inc(stored, 16)
            sp.dma_start(h_tok[0:1, 0, 64:128], zeros[0:1, 64:128]).then_inc(h_first_in, 16)
            sp.wait_ge(zero_row, 16)
            sp.wait_ge(stored, 16)

            def load_group(G):
                need(sp, ht_done, G)
                sp.dma_start(h_tok[:, :, 0:64], tiles_of(group_in[G, 1:1 + GTOK, 0:64])).then_inc(h_in, 16)
                sp.dma_start(h_tok[:, :, 64:128], tiles_of(group_in[G, 0:GTOK, 64:128])).then_inc(h_in, 16)

            def load_tables(G):
                need(sp, tab_ready, GT * G)
                sp.dma_start(tab_raw[:, :, :], tables[G]).then_inc(tab_in, 16)
                sp.dma_start(head_scale[:, :], head_scales[G:G + 1].broadcast_to([P, TABW]) if isinstance(G, int)
                             else head_scales[bass.ds(G, 1), :].broadcast_to([P, TABW])).then_inc(tab_in, 16)

            def load_residual(G, j):
                need(sp, xa_ready, GT * (G - 1) + j + 1)
                sp.dma_start(x_res[:, j, :], group_in[G, 1 + j * P:1 + (j + 1) * P, :]).then_inc(res_in[j], 16)

            def load_h2(F):
                need(sp, xa_ready, GT * F + GT)
                need(sp, early_moved, F + 1)
                sp.dma_start(h2[0:1, :, 64:128], x_attn[P - 1:P, 0:GT, 64:128]).then_inc(h2_in, 16)
                sp.dma_start(h2[:, :, 0:64], x_attn[:, 1:GT + 1, 0:64]).then_inc(h2_in, 16)
                sp.dma_start(h2[1:113, :, 64:128], x_attn[0:112, 1:GT + 1, 64:128]).then_inc(h2_in, 16)
                sp.dma_start(h2[113:128, :, 64:128], x_attn[112:127, 1:GT + 1, 64:128]).then_inc(h2_in, 16)

            def load_carry(F):
                need(sp, h2_in, 64 * (F + 1))
                ends = isinstance(F, int) and F % GROUPS == GROUPS - 1
                last = zeros[P - 1:P, 64:128] if ends else x_attn[P - 1:P, GT, 64:128]
                sp.dma_start(x_attn[P - 1:P, 0, 64:128], last).then_inc(carry_in, 16)

            def store(F, layer):
                if layer == 0:
                    need(sp, y_ready, F + 1)
                    sp.dma_start(tiles_of(group_in[F + GROUPS, 1:1 + GTOK, :]), y[:, :, :]).then_inc(stored, 16)
                    if not (isinstance(F, int) and F == GROUPS - 1):
                        sp.dma_start(group_in[F + GROUPS + 1, 0:1, :], y[P - 1:P, GT - 1, :]).then_inc(stored, 16)
                else:
                    need(sp, out_ready, F - GROUPS + 1)
                    sp.dma_start(by_group(out)[F - GROUPS], y_out[:, :, :]).then_inc(stored, 16)
                need(sp, carry_in, 16 * (F + 1))

            def store_mixed(g):
                sp.dma_start(tiles_of(group_in[g, 1:1 + GTOK, :]), group_tiles(normed, g)).then_inc(xf_stored, 16)
                if not (isinstance(g, int) and g == GROUPS - 1):
                    src = normed[P - 1:P, GT * g + GT - 1, :]
                    sp.dma_start(group_in[g + 1, 0:1, :], src).then_inc(xf_stored, 16)

            sp.wait_ge(xf_ready, 1)
            sp.dma_start(h_tok[1:113, :, 64:128], normed[0:112, 0:GT, 64:128]).then_inc(h_first_in, 16)
            sp.dma_start(h_tok[113:128, :, 64:128], normed[112:127, 0:GT, 64:128]).then_inc(h_first_in, 16)
            sp.dma_start(h_tok[0:1, 1:GT, 64:128], normed[P - 1:P, 0:GT - 1, 64:128]).then_inc(h_first_in, 16)
            sp.dma_start(h_tok[:, :, 0:64], normed[:, 0:GT, 0:64]).then_inc(h_first_in, 16)
            store_mixed(0)
            sp.dma_start(x_res[:, :, :], normed[:, 0:GT, :]).then_inc(x_res_first, 16)
            with sp.Fori(1, GROUPS - 1) as g:
                need(sp, xf_ready, g + 1)
                store_mixed(g)
            sp.wait_ge(xf_ready, GROUPS)
            store_mixed(GROUPS - 1)
            sp.wait_ge(xf_stored, 16 * (2 * GROUPS - 1))

            def body(G, layer):
                number = isinstance(G, int)
                for j in range(GT):
                    cur = At(G, j, 0, layer)
                    if j == 0 and not (number and not 0 <= G < LAST - 1):
                        load_tables(G + 1)
                        if layer == 0 or (number and G <= GROUPS):
                            need(sp, stored, 16 + 32 * (G - 1))
                        else:
                            sp.wait_ge(stored, FIRST_LAYER)
                        load_group(G + 1)
                    ffn = j == 0 and not (number and G < 1)
                    if ffn:
                        load_h2(G - 1)
                    if cur.valid and not (number and cur.t < GT):
                        load_residual(cur.group, cur.slot)
                    if cur.valid:
                        need(sp, pv_done, cur.t - 3)
                        need(sp, v_saved, cur.t + 1)
                        sp.dma_start(v_mid[cur.slot][0:64, :], v_tok[(cur.slot - 1) % GT][64:128, :]).then_inc(v_mid_in[cur.slot], 16)
                        sp.dma_start(v_mid[cur.slot][64:128, :], v_tok[cur.slot][0:64, :]).then_inc(v_mid_in[cur.slot], 16)
                    if ffn:
                        load_carry(G - 1)
                        if number and G == LAST:
                            store(LAST - 2, DEPTH - 1)
                if not (number and (G < 1 or G == LAST - 1)):
                    store(G - 1, (G - 1) // GROUPS if number else layer)

            passes(sp, body)
            sp.wait_ge(stored, FIRST_LAYER + 16 * GROUPS)

        @block.gpsimd
        def _(pool):
            pool.memset(zeros[:, :], 0.0).then_inc(zeros_ready, 1)
            pool.memset(q_even[:, :, :], 0.0).then_inc(init_done, 1)
            pool.memset(q_odd[:, :, :], 0.0).then_inc(init_done, 1)
            pool.memset(k_t[:, :, 0:WINDOW], 0.0).then_inc(k_carried, 1)
            pool.memset(v_tok[GT - 1][:, :], 0.0).then_inc(init_done, 1)
            pool.memset(x_attn[:, 0, :], 0.0).then_inc(init_done, 1)
            pool.memset(gated[:, 2, :], 1.0).then_inc(init_done, 1)
            pool.wait_ge(w_mix_high, 1)
            pool.tensor_tensor(w_hg_lo[:, :], w_hg_raw[:, :], w_hg_hi[:, :].bitcast(F32), ALU.subtract).then_inc(w_mix_split, 1)
            def low_parts(l):
                pool.wait_ge(w_high, 2 * l + 2)
                pool.tensor_tensor(wqkv_lo[l][:, :], wqkv_raw[l][:, :], wqkv_hi[l][:, :].bitcast(F32), ALU.subtract).then_inc(w_split, 1)
                pool.tensor_tensor(w1_lo[l][:, :], w1_raw[l][:, :], w1_hi[l][:, :].bitcast(F32), ALU.subtract).then_inc(w_split, 1)

            def add_mixed(g):
                if 0 < g < GROUPS - 1:
                    pool.wait_ge(mix_act, g)
                else:
                    pool.wait_ge(mix_done, 1 if g == 0 else 2)
                pool.tensor_tensor(group_tiles(x_in, g), group_tiles(x_in, g), group_tiles(normed, g), ALU.add).then_inc(x1_ready, 1)

            low_parts(0)
            for g in range(GROUPS):
                add_mixed(g)

            def scale_table(G, j):
                pool.wait_ge(tab_in, 32 * (G + 1))
                pool.tensor_tensor(tab[:, j, :], tab_raw[:, j, :], head_scale[:, :], ALU.mult).then_inc(tab_ready, 1)

            for j in range(GT):
                scale_table(0, j)
            low_parts(1)

            def body(G, layer):
                number = isinstance(G, int)
                for j in range(GT):
                    cur = At(G, j, 0, layer)
                    t = cur.t
                    if cur.valid:
                        pool.wait_ge(q_rot, 2 * (t + 1))
                        pool.wait_ge(k_rot, 2 * (t + 1))
                        need(pool, kt_done, t)
                        pool.tensor_tensor(rot[:, :, 0:32], rot_cos[:, :, 0:32], rot_sin[:, :, 32:64], ALU.add).then_inc(rot_added, 1)
                        pool.tensor_tensor(rot[:, :, 32:64], rot_cos[:, :, 32:64], rot_sin[:, :, 0:32], ALU.add).then_inc(rot_added, 1)
                    if not (number and not 0 <= G < LAST - 1):
                        scale_table(G + 1, j)
                    if cur.valid:
                        pool.wait_ge(rn_ready, t + 1)
                        pool.wait_ge(rot_added, 2 * (t + 1))
                        pool.tensor_tensor(rot[:, :, :], rot[:, :, :],
                                           rn[:, 0:2 * HEADS].unsqueeze(2).broadcast_to([P, 2 * HEADS, DH]),
                                           ALU.mult).then_inc(rot_scaled, 1)
                    if cur.valid and cur.slot == 0 and not (number and G < 0):
                        pool.wait_ge(k_saved, t)
                        pool.wait_ge(s_done, 2 * (t - GT + 1))
                        settle(pool)
                        if cur.first:
                            pool.memset(k_t[:, :, 0:WINDOW], 0.0).then_inc(k_carried, 1)
                        else:
                            pool.tensor_copy(k_t[:, :, 0:WINDOW], k_t[:, :, GTOK:GTOK + WINDOW]).then_inc(k_carried, 1)
                    if j == 3 and (G > GROUPS if number else layer == DEPTH - 1):
                        g = G - 1 - GROUPS
                        pool.wait_ge(y_normed, g + 1)
                        pool.tensor_tensor(y_out[:, :, :], y_out[:, :, :], group_tiles(x_in, g), ALU.add).then_inc(out_ready, 1)
            passes(pool, body)

        W_IN = 16 * DEPTH * 12

        @block.tensor
        def _(pe):
            def product3(out_ap, lhs, rhs, lhs_lo, rhs_lo, rhs_lo_ready=None):
                pe.matmul(out_ap, lhs, rhs, start=True, stop=False)
                pe.matmul(out_ap, lhs_lo, rhs, start=False, stop=False)
                if rhs_lo_ready:
                    pe.wait_ge(*rhs_lo_ready)
                return pe.matmul(out_ap, lhs, rhs_lo, start=False, stop=True)

            def mixer_transpose(g):
                need(pe, xn_ready, g + 1)
                for k in range(GT):
                    last = pe.transpose(qt_bank[:, k * P:(k + 1) * P], normed[:, GT * g + k, :], ident)
                last.then_inc(xnt_done, 1)

            def mixer_project(g):
                pe.wait_ge(xnt_hi, g + 1)
                need(pe, sig_done, 3 * g)
                need(pe, hidden_read, g)
                for n, b in enumerate((q_bank, k_bank)):
                    cols = slice(n * P, (n + 1) * P)
                    product3(b[:, :], w_hg_hi[:, cols], act_t_hi[:, :], w_hg_lo[:, cols], act_t_lo[:, :],
                             (xnt_lo, g + 1)).then_inc(hg_done, 1)

            def mixer_out(g):
                pe.wait_ge(scan_done, g + 1)
                for k in range(GT):
                    last = pe.matmul(mix_out[:, g, k * P:(k + 1) * P], scan_h[:, k * P:(k + 1) * P], w_out_sb[:, :],
                                     start=True, stop=True)
                last.then_inc(mixed, 1)

            pe.wait_ge(consts_in, 16)
            mixer_transpose(0)
            pe.wait_ge(w_mix_in, 32)
            pe.wait_ge(w_mix_high, 1)
            pe.wait_ge(w_mix_split, 1)
            mixer_project(0)
            for g in range(GROUPS - 1):
                mixer_transpose(g + 1)
                mixer_project(g + 1)
                mixer_out(g)
            mixer_out(GROUPS - 1)
            pe.wait_ge(mix_done, 2)
            pe.wait_ge(mix_act, GROUPS - 2)

            def transpose_inputs(G):
                if isinstance(G, int) and G == 0:
                    pe.wait_ge(h_first_in, 16 * 5)
                else:
                    pe.wait_ge(h_in, 32 * G)
                for k in range(GT):
                    last = pe.transpose(ht_bank[:, k * P:(k + 1) * P], h_tok[:, k, :], ident)
                last.then_inc(ht_done, 1)

            def transpose_qk(a):
                pe.wait_ge(rot_scaled, a.t + 1)
                for half, (b, ready) in enumerate(((qt_bank, qt_done), (kt_bank, kt_done))):
                    for p in range(PAIRS):
                        h = half * HEADS + 2 * p
                        last = pe.transpose(b[:, p * P:(p + 1) * P], rot[:, h:h + 2, :].rearrange("p h d -> p (h d)"), ident)
                    last.then_inc(ready, 1)

            def transpose_o(a):
                pe.wait_ge(o_ready, a.t + 1)
                need(pe, xa_ready, a.t)
                for c in range(4):
                    last = pe.transpose(misc_bank[:, c * P:(c + 1) * P], o_tok[:, c * P:(c + 1) * P], ident)
                last.then_inc(ot_done, 1)

            def project_qkv(a):
                pe.wait_ge(ht_hi, a.group + 1)
                pe.wait_ge(ht_lo, a.group + 1)
                need(pe, q_rot, 2 * a.t)
                need(pe, k_rot, 2 * a.t)
                need(pe, squared, 2 * a.t)
                tok = slice(a.slot * P, (a.slot + 1) * P)
                for n, (b, ready) in enumerate(((q_bank, q_done), (k_bank, k_done), (v_bank, v_done))):
                    w = slice(n * INNER, (n + 1) * INNER)
                    if n == 2:
                        need(pe, v_saved, a.t)
                        need(pe, o_ready, a.t - 2)
                    product3(b[:, :], act_t_hi[:, tok], wqkv_hi[a.layer][:, w],
                             act_t_lo[:, tok], wqkv_lo[a.layer][:, w]).then_inc(ready, 1)

            def transpose_probs(a, half):
                pe.wait_ge(exp_done, 2 * a.t + 1 + half)
                for h in range(4 * half, 4 * half + 4):
                    last = pe.transpose(pt_bank[half][:, (h % 4) * P:(h % 4 + 1) * P], probs[:, h, :], ident)
                last.then_inc(pt_done, 1)

            def project_out(a):
                pe.wait_ge(ot_saved, a.t + 1)
                for c in range(4):
                    last = pe.matmul(misc_bank[:, 0:DIM], o_t[:, c, :], wo_sb[a.layer][:, c, :],
                                     start=(c == 0), stop=(c == 3))
                last.then_inc(wo_done, 1)

            def scores(a, half):
                if half == 0 and a.slot == 0:
                    pe.wait_ge(k_carried, a.group + 1)
                need(pe, (pt_saved0, pt_saved1)[half], a.t)
                b = s_bank[half]
                pe.matmul(b[:, :], ident_bf[:, :], mask_bf[1 if a.first else 0][:, :], start=True, stop=True)
                for h in range(4 * half, 4 * half + 4):
                    q, col = (q_even, q_odd)[h % 2][:, h // 2, :], (h % 4) * P
                    keys = k_t[:, h // 2, a.slot * P:]
                    for low in (0, 64):
                        last = pe.matmul(b[low:low + 64, col:col + P], q[:, low:low + 64], keys[:, low:low + P],
                                         start=False, stop=True, skip_group_check=True)
                last.then_inc(s_done, 1)

            def mix_values(a):
                pe.wait_ge(pt_saved0, a.t + 1)
                pe.wait_ge(pt_saved1, a.t + 1)
                pe.wait_ge(v_mid_in[a.slot], 32 * (a.group + 1))
                need(pe, o_ready, a.t)
                pe.wait_ge(v_saved, min(a.t + 3, DEPTH * TILES) if isinstance(a.t, int) else a.t + 3)
                for h in range(HEADS):
                    cols = slice(h * DH, (h + 1) * DH)
                    for low, v in ((0, v_mid[a.slot]), (64, v_tok[a.slot])):
                        last = pe.matmul(o_bank[low:low + 64, cols], probs_t[:, h, low:low + 64], v[:, cols],
                                         start=True, stop=True)
                last.then_inc(pv_done, 1)

            def transpose_h2(F):
                pe.wait_ge(h2_ready, F + 1)
                for k in range(GT):
                    last = pe.transpose(h2t_bank[:, k * P:(k + 1) * P], h2[:, k, :], ident)
                last.then_inc(h2t_done, 1)

            def feed_forward(F, layer, t_now):
                taken = min(t_now, DEPTH * TILES) if isinstance(F, int) else t_now
                pe.wait_ge(h2t_saved, 2 * F + 1)
                for c, (c0, cn) in enumerate(CHUNKS):
                    if c == 1:
                        pe.wait_ge(q_rot, 2 * taken)
                        pe.wait_ge(k_rot, 2 * taken)
                        pe.wait_ge(squared, 2 * taken)
                    if c == 2:
                        pe.wait_ge(ot_saved, min(t_now - 3, DEPTH * TILES) if isinstance(F, int) else t_now - 3)
                        pe.wait_ge(xa_ready, min(t_now - 4, DEPTH * TILES) if isinstance(F, int) else t_now - 4)
                        pe.wait_ge(o_ready, min(t_now - 2, DEPTH * TILES) if isinstance(F, int) else t_now - 2)
                    for part, b in enumerate(up_bank[c]):
                        w = slice(part * HID + c0, part * HID + c0 + cn)
                        last = product3(b[0:cn, :], w1_hi[layer][:, w], h2_hi[:, :], w1_lo[layer][:, w], h2_lo[:, :],
                                        (h2_split, F + 1) if c == 0 and part == 0 else None)
                    last.then_inc(up_done, 1)
                for c, (c0, cn) in enumerate(CHUNKS):
                    pe.wait_ge(gated_done, 3 * F + c + 1)
                    for k in range(GT):
                        rows = cn + 1 if c == 2 else cn
                        last = pe.matmul(y_bank[:, k * P:(k + 1) * P], gated[0:rows, c, k * P:(k + 1) * P],
                                         w2_sb[layer][0:rows, c, :], start=(c == 0 and k == 0), stop=(c == 2),
                                         skip_group_check=True)
                last.then_inc(down_done, 1)

            pe.wait_ge(init_done, 5)
            pe.wait_ge(const_bf, 3)
            pe.wait_ge(w_ffn_in, W_IN)
            pe.wait_ge(w_high, 2)
            pe.wait_ge(w_split, 2)
            transpose_inputs(0)

            def body(G, layer):
                number = isinstance(G, int)
                if number and G == GROUPS - 1:
                    pe.wait_ge(w_high, 2 * DEPTH)
                    pe.wait_ge(w_split, 2 * DEPTH)
                for j in range(GT):
                    cur, prev, mid, done, after = (At(G, j, back, layer) for back in range(5))
                    ffn = j == 2 and not (number and G < 1)
                    if cur.valid:
                        project_qkv(cur)
                    if after.valid:
                        project_out(after)
                    if mid.valid:
                        transpose_probs(mid, 0)
                        transpose_probs(mid, 1)
                    if prev.valid:
                        if j == 3:
                            pe.wait_ge(y_read, G + 1)
                        transpose_qk(prev)
                    if done.valid:
                        transpose_o(done)
                    if mid.valid:
                        mix_values(mid)
                    if prev.valid:
                        pe.wait_ge(q_saved, 2 * (prev.t + 1))
                        pe.wait_ge(k_saved, prev.t + 1)
                    if j == 0 and not (number and not 0 <= G < LAST - 1):
                        transpose_inputs(G + 1)
                    if ffn:
                        transpose_h2(G - 1)
                    if prev.valid:
                        scores(prev, 0)
                        scores(prev, 1)
                    if ffn:
                        feed_forward(G - 1, (G - 1) // GROUPS if number else layer, cur.t + 1 if not number
                                     else min(cur.t + 1, DEPTH * TILES + 4))

            passes(pe, body)

        @block.scalar
        def _(act):
            act.wait_ge(w_mix_in, 32)
            act.copy(w_hg_hi[:, :], w_hg_raw[:, :]).then_inc(w_mix_high, 1)

            def high_parts(l):
                act.copy(wqkv_hi[l][:, :], wqkv_raw[l][:, :]).then_inc(w_high, 1)
                act.copy(w1_hi[l][:, :], w1_raw[l][:, :]).then_inc(w_high, 1)

            def mixer(g):
                act.wait_ge(xnt_done, g + 1)
                need(act, hg_done, 2 * g)
                act.copy(act_t_hi[:, :], qt_bank[:, :]).then_inc(xnt_hi, 1)
                act.wait_ge(hg_done, 2 * g + 2)
                need(act, scan_done, g)
                act.activation(sig_hidden[:, :], q_bank[:, :], ACT.Sigmoid).then_inc(sig_done, 1)
                act.activation(sig_gate[:, :], k_bank[:, :], ACT.Sigmoid).then_inc(sig_done, 1)
                act.activation(coef_a[:, :], k_bank[:, :], ACT.Sigmoid, scale=-1.0).then_inc(sig_done, 1)

            mixer(0)
            with act.Fori(1, GROUPS) as g:
                mixer(g)
            act.wait_ge(w_big_in, 32 * DEPTH)
            for l in range(DEPTH):
                high_parts(l)
            act.wait_ge(consts_in, 16)
            act.copy(ident_bf[:, :], ident).then_inc(const_bf, 1)
            for n, m in enumerate(mask_bf):
                src = const[:, (n + 1) * P:(n + 2) * P]
                act.copy(m[:, :].rearrange("p (h k) -> p h k", h=GT),
                         src.unsqueeze(1).broadcast_to([P, GT, P])).then_inc(const_bf, 1)
            act.wait_ge(w_ffn_in, W_IN)

            def group_normalise(g, src):
                for k in range(GT):
                    t = GT * g + k
                    last = act.activation(normed[:, t, :], src(k), ACT.Identity, bias=shift[:, t:t + 1], scale=rn[:, t:t + 1])
                return last

            act.wait_ge(shift_ready, 1)
            for g in range(1, GROUPS - 1):
                group_normalise(g, lambda k: mix_out[:, g, k * P:(k + 1) * P]).then_inc(mix_act, 1)

            def save_inputs(G):
                act.wait_ge(ht_done, G + 1)
                need(act, v_done, GT * G)
                act.copy(act_t_hi[:, :], ht_bank[:, :]).then_inc(ht_hi, 1)

            save_inputs(0)
            act.wait_ge(shift_ready, 2)
            for g in range(1, GROUPS):
                group_normalise(g, lambda k: x_in[:, GT * g + k, :]).then_inc(xf_ready, 1)

            def exponentials(a, half):
                act.wait_ge(max_ready, 2 * a.t + 1 + half)
                if half == 0:
                    need(act, pt_done, 2 * a.t)
                    need(act, o_ready, a.t - 1)
                for h in range(4 * half, 4 * half + 4):
                    last = act.activation(probs[:, h, :], s_bank[half][:, (h % 4) * P:(h % 4 + 1) * P], ACT.Exp,
                                          bias=neg_max[a.par][:, h:h + 1], accum_out=row_sum[a.par][:, h:h + 1])
                last.then_inc(exp_done, 1)

            def body(G, layer):
                number = isinstance(G, int)
                for j in range(GT):
                    cur, prev, mid, done = (At(G, j, back, layer) for back in range(4))
                    if mid.valid:
                        exponentials(mid, 0)
                        exponentials(mid, 1)
                    if cur.valid:
                        act.wait_ge(v_done, cur.t + 1)
                        need(act, pv_done, cur.t - 3)
                        if not (number and cur.t < GT):
                            moved = At(G, j, 3, layer)
                            act.wait_ge(v_mid_in[moved.slot], 32 * (moved.group + 1))
                        act.copy(v_tok[cur.slot][:, :], v_bank[:, :]).then_inc(v_saved, 1)
                        need(act, rn_ready, cur.t)
                        for n, (b, read) in enumerate(((q_bank, q_rot), (k_bank, k_rot))):
                            act.wait_ge(read, 2 * (cur.t + 1))
                            act.activation(sq[:, n * INNER:(n + 1) * INNER], b[:, :], ACT.Square).then_inc(squared, 1)
                    if mid.valid:
                        act.wait_ge(pt_done, 2 * mid.t + 1)
                        need(act, pv_done, mid.t)
                        act.copy(probs_t[:, 0:4, :], pt_bank[0][:, :].rearrange("p (h t) -> p h t", h=4)).then_inc(pt_saved0, 1)
                        if j == 1:
                            act.wait_ge(pt_done, 2 * mid.t + 2)
                            act.copy(probs_t[:, 4:8, :], pt_bank[1][:, :].rearrange("p (h t) -> p h t", h=4)).then_inc(pt_saved1, 1)
                    if prev.valid:
                        act.wait_ge(qt_done, prev.t + 1)
                        need(act, s_done, 2 * prev.t)
                        act.copy(q_even[0:64, :, :], qt_bank[0:64, :].rearrange("p (c t) -> p c t", c=PAIRS)).then_inc(q_saved, 1)
                        act.copy(q_odd[64:128, :, :], qt_bank[64:128, :].rearrange("p (c t) -> p c t", c=PAIRS)).then_inc(q_saved, 1)
                        act.wait_ge(kt_done, prev.t + 1)
                        if prev.slot == GT - 1:
                            act.wait_ge(k_carried, prev.group + 1)
                        act.copy(k_t[:, :, WINDOW + prev.slot * P:WINDOW + (prev.slot + 1) * P],
                                 kt_bank[:, :].rearrange("p (c t) -> p c t", c=PAIRS)).then_inc(k_saved, 1)
                    if done.valid:
                        act.wait_ge(ot_done, done.t + 1)
                        need(act, wo_done, done.t)
                        act.copy(o_t[:, :, :], misc_bank[:, :].rearrange("p (c t) -> p c t", c=4)).then_inc(ot_saved, 1)
                    if j == 0 and not (number and not 0 <= G < LAST - 1):
                        save_inputs(G + 1)
                    if j == 2 and not (number and G < 1):
                        F = G - 1
                        l = F // GROUPS if number else layer
                        act.wait_ge(h2t_done, F + 1)
                        for dst in (h2_hi, h2_t):
                            act.activation(dst[:, :], h2t_bank[:, :], ACT.Identity, bias=lngb[l][:, 1:2],
                                           scale=lngb[l][:, 0:1]).then_inc(h2t_saved, 1)
                        for c, (c0, cn) in enumerate(CHUNKS):
                            act.wait_ge(up_done, 3 * F + c + 1)
                            act.activation(gelu_g[0:cn, c, :], up_bank[c][1][0:cn, :], ACT.Gelu,
                                           bias=b1_sb[l][0:cn, 3 + c:4 + c]).then_inc(gelu_done, 1)

            passes(act, body)

        @block.vector
        def _(dve):
            steps = Steps(dve, dve_chain)
            link = steps.link

            def newton_seed(cols):
                steps.catch_up()
                steps.mark(dve.tensor_scalar(rn[:, cols].bitcast(I32), nw_x[:, cols].bitcast(I32), -0.5,
                                               float(RSQRT_SEED - 2 ** 30 - 2 ** 22), ALU.mult, ALU.add))

            def cubic_round(cols):
                steps.catch_up()
                link(dve.tensor_tensor(nw_t[:, cols], rn[:, cols], rn[:, cols], ALU.mult))
                link(dve.tensor_tensor(nw_t[:, cols], nw_t[:, cols], nw_x[:, cols], ALU.mult))
                link(dve.scalar_tensor_tensor(nw_t[:, cols], nw_t[:, cols], 5 / 3, nw_t[:, cols], ALU.add, ALU.mult))
                steps.mark(dve.scalar_tensor_tensor(rn[:, cols], nw_t[:, cols], 1.25, rn[:, cols], ALU.add, ALU.mult))

            def newton_square(cols):
                steps.catch_up()
                steps.mark(dve.scalar_tensor_tensor(nw_t[:, cols], rn[:, cols], 27 / 8, rn[:, cols], ALU.mult, ALU.mult))

            def newton_product(cols):
                steps.catch_up()
                steps.mark(dve.tensor_tensor(nw_t[:, cols], nw_t[:, cols], nw_x[:, cols], ALU.mult))

            def newton_update(cols):
                steps.catch_up()
                return dve.scalar_tensor_tensor(rn[:, cols], nw_t[:, cols], 9 / 4, rn[:, cols], ALU.add, ALU.mult)

            def newton_round(cols):
                newton_square(cols)
                newton_product(cols)
                return newton_update(cols)

            def group_stats(g, src):
                for k in range(GT):
                    last = dve.bn_stats(stats[:, GT * g + k, :], src(k))
                return last

            def inverse_deviations(g0, g1):
                cols = slice(GT * g0, GT * g1)
                for t in range(GT * g0, GT * g1):
                    last = dve.bn_aggr(mean_var[:, t, :], stats[:, t, :])
                link(last)
                steps.mark(dve.tensor_scalar(nw_x[:, cols], mean_var[:, cols, 1], LN_EPS, -0.5, ALU.add, ALU.mult))
                newton_seed(cols)
                cubic_round(cols)
                steps.mark(newton_round(cols))
                steps.catch_up()

            def group_shift(g0, g1):
                cols = slice(GT * g0, GT * g1)
                dve.scalar_tensor_tensor(shift[:, cols], mean_var[:, cols, 0], -1.0, rn[:, cols],
                                         ALU.mult, ALU.mult).then_inc(shift_ready, 1)

            def group_normalise(g, src, at=None):
                for k in range(GT):
                    t = GT * (g if at is None else at) + k
                    last = dve.tensor_scalar(normed[:, GT * g + k, :], src(k), mean_var[:, t, 0:1], rn[:, t:t + 1],
                                             ALU.subtract, ALU.mult)
                return last

            def mixer_split(g):
                dve.wait_ge(xnt_hi, g + 1)
                dve.tensor_tensor(act_t_lo[:, :], qt_bank[:, :], act_t_hi[:, :].bitcast(F32), ALU.subtract).then_inc(xnt_lo, 1)

            def mixer_values(g):
                dve.wait_ge(sig_done, 3 * g + 3)
                link(dve.tensor_scalar(sig_hidden[:, :], sig_hidden[:, :], 0.5, None, ALU.min))
                dve.scalar_tensor_tensor(value_b[:, :], q_bank[:, :], 0.0, sig_hidden[:, :], ALU.max, ALU.add).then_inc(hidden_read, 1)

            def mixer_scan(g, carry):
                dve.wait_ge(hidden_read, g + 1)
                link(dve.tensor_tensor(value_b[:, :], value_b[:, :], sig_gate[:, :], ALU.mult))
                need(dve, mixed, g)
                dve.tensor_tensor_scan(scan_h[:, :], coef_a[:, :], value_b[:, :], scan_carry[:, 0:1] if carry else 0.0,
                                       ALU.mult, ALU.add).then_inc(scan_done, 1)
                dve.wait_ge(scan_done, g + 1)
                dve.tensor_copy(scan_carry[:, :], scan_h[:, GTOK - 1:GTOK])

            tile_of = lambda g: lambda k: x_in[:, GT * g + k, :]
            out_of = lambda g: lambda k: mix_out[:, g, k * P:(k + 1) * P]
            dve.wait_ge(x_in_done[0], 16)
            link(group_stats(0, tile_of(0)))
            inverse_deviations(0, 1)
            group_normalise(0, tile_of(0)).then_inc(xn_ready, 1)
            for g in range(1, GROUPS):
                dve.wait_ge(x_in_done[g], 16)
                last = group_stats(g, tile_of(g))
            link(last)
            mixer_split(0)
            inverse_deviations(1, GROUPS)
            group_normalise(1, tile_of(1)).then_inc(xn_ready, 1)
            mixer_values(0)
            mixer_split(1)
            for g in range(2, GROUPS):
                group_normalise(g, tile_of(g)).then_inc(xn_ready, 1)
            mixer_scan(0, False)
            for g in range(1, GROUPS):
                mixer_values(g)
                if g + 1 < GROUPS:
                    mixer_split(g + 1)
                mixer_scan(g, True)
                last = group_stats(g - 1, out_of(g - 1))
            link(last)
            ahead, spare = GROUPS - 1, GROUPS
            inverse_deviations(0, ahead)
            group_shift(1, ahead)
            group_normalise(0, out_of(0)).then_inc(mix_done, 1)
            dve.wait_ge(mixed, GROUPS)
            group_stats(ahead, out_of(ahead))
            dve.wait_ge(x1_ready, 1)
            link(group_stats(spare, tile_of(0)))
            inverse_deviations(ahead, spare + 1)
            group_normalise(0, tile_of(0), at=spare).then_inc(xf_ready, 1)
            group_normalise(ahead, out_of(ahead)).then_inc(mix_done, 1)
            for g in range(1, GROUPS):
                dve.wait_ge(x1_ready, g + 1)
                last = group_stats(g, tile_of(g))
            link(last)
            inverse_deviations(1, GROUPS)
            group_shift(1, GROUPS)

            def split_inputs(G):
                dve.wait_ge(ht_hi, G + 1)
                need(dve, v_done, GT * G)
                dve.tensor_tensor(act_t_lo[:, :], ht_bank[:, :], act_t_hi[:, :].bitcast(F32), ALU.subtract).then_inc(ht_lo, 1)

            split_inputs(0)

            def rotate(a):
                dve.wait_ge(tab_ready, a.t + 1)
                need(dve, rot_added, 2 * a.t)
                for n, (b, ready, done) in enumerate(((q_bank, q_done, q_rot), (k_bank, k_done, k_rot))):
                    dve.wait_ge(ready, a.t + 1)
                    src = b[:, :].rearrange("p (h d) -> p h d", h=HEADS)
                    for m, dst in enumerate((rot_cos, rot_sin)):
                        table = tab[:, a.slot, (2 * n + m) * DH:(2 * n + m + 1) * DH]
                        dve.tensor_tensor(dst[:, n * HEADS:(n + 1) * HEADS, :], src,
                                          table.unsqueeze(1).broadcast_to([P, HEADS, DH]), ALU.mult).then_inc(done, 1)

            def sum_squares(a):
                dve.wait_ge(squared, 2 * (a.t + 1))
                link(dve.tensor_reduce(ss[:, :], sq[:, :].rearrange("p (h d) -> p h d", h=2 * HEADS), AX.X, ALU.add))
                steps.mark(dve.tensor_scalar(nw_x[:, 0:2 * HEADS], ss[:, :], NORM_FLOOR, -0.5, ALU.max, ALU.mult))

            def variances(src):
                settle(dve)
                for k in range(GT):
                    last = dve.bn_stats(stats[:, k, :], src[:, k, :])
                link(last)
                settle(dve)
                for k in range(GT):
                    last = dve.bn_aggr(mean_var[:, k, :], stats[:, k, :])
                link(last)
                steps.mark(dve.tensor_scalar(nw_x[:, 2 * HEADS:], mean_var[:, 0:GT, 1], LN_EPS, -0.5, ALU.add, ALU.mult))

            def normalise_tiles(dst, src):
                steps.catch_up()
                for k in range(GT):
                    col = 2 * HEADS + k
                    last = dve.tensor_scalar(dst[:, k, :], src[:, k, :], mean_var[:, k, 0:1], rn[:, col:col + 1],
                                             ALU.subtract, ALU.mult)
                return last

            def save_probs(a):
                dve.wait_ge(pt_done, 2 * a.t + 2)
                need(dve, pv_done, a.t)
                dve.tensor_copy(probs_t[:, 4:8, :], pt_bank[1][:, :].rearrange("p (h t) -> p h t", h=4)).then_inc(pt_saved1, 1)

            def add_residual(a):
                dve.wait_ge(wo_done, a.t + 1)
                if isinstance(a.t, int) and a.t < GT:
                    dve.wait_ge(x_res_first, 16)
                else:
                    dve.wait_ge(res_in[a.slot], 16 * a.group)
                dst = x_early[:, a.slot, :] if a.slot < 2 else x_attn[:, a.slot + 1, :]
                dve.tensor_tensor(dst, misc_bank[:, 0:DIM], x_res[:, a.slot, :], ALU.add).then_inc(xa_ready, 1)

            def row_max(a, half):
                dve.wait_ge(s_done, 2 * a.t + 1 + half)
                need(dve, exp_done, 2 * (a.t - 1))
                src = s_bank[half][:, :].rearrange("p (h k) -> p h k", h=4)
                dve.tensor_reduce(neg_max[a.par][:, 4 * half:4 * half + 4], src, AX.X, ALU.max, negate=True).then_inc(max_ready, 1)

            def invert_sums(a):
                dve.wait_ge(exp_done, 2 * a.t + 2)
                steps.mark(dve.reciprocal(inv_sum[:, :], row_sum[a.par][:, :]))

            def divide_o(a):
                steps.catch_up()
                dve.wait_ge(pv_done, a.t + 1)
                need(dve, ot_done, a.t)
                dve.tensor_tensor(o_tok[:, :].rearrange("p (h d) -> p h d", h=HEADS),
                                  o_bank[:, :].rearrange("p (h d) -> p h d", h=HEADS),
                                  inv_sum[:, :].unsqueeze(2).broadcast_to([P, HEADS, DH]), ALU.mult).then_inc(o_ready, 1)

            def split_h2(F):
                dve.wait_ge(h2t_saved, 2 * (F + 1))
                dve.tensor_tensor(h2_lo[:, :], h2_t[:, :], h2_hi[:, :].bitcast(F32), ALU.subtract).then_inc(h2_split, 1)

            def gate(F, layer, c, cn):
                dve.wait_ge(gelu_done, 3 * F + c + 1)
                dve.scalar_tensor_tensor(gated[0:cn, c, :], up_bank[c][0][0:cn, :], b1_sb[layer][0:cn, c:c + 1],
                                         gelu_g[0:cn, c, :], ALU.add, ALU.mult).then_inc(gated_done, 1)

            def place_early(G):
                if not (isinstance(G, int) and G >= LAST):
                    dve.wait_ge(xa_ready, GT * G + 2)
                    dve.tensor_copy(x_attn[:, 1:3, :], x_early[:, :, :]).then_inc(early_moved, 1)

            def finish_group(F, layer):
                dve.wait_ge(down_done, F + 1)
                dve.wait_ge(stored, 16 + 32 * F if layer == 0 else FIRST_LAYER)
                add = dve.tensor_tensor(y[:, :, :], y_bank[:, :].rearrange("p (k d) -> p k d", k=GT),
                                        x_attn[:, 1:GT + 1, :], ALU.add)
                add.then_inc(y_read, 1)
                dve.wait_ge(y_read, F + 2)
                dve.wait_ge(carry_in, 16 * (F + 1))
                place_early(F + 1)
                if layer == 0:
                    dve.nop().then_inc(y_ready, 1)

            def body(G, layer):
                number = isinstance(G, int)
                for j in range(GT):
                    cur, prev, mid, done, after = (At(G, j, back, layer) for back in range(5))
                    norm, ffn = (j == n and not (number and G < 1) for n in (1, 2))
                    final = j == 3 and (GROUPS < G != LAST - 1 if number else layer == DEPTH - 1)
                    if mid.valid and j != 3:
                        row_max(mid, 0)
                    if prev.valid and j in (1, 2):
                        newton_product(last_cols)
                    if done.valid and j != 3:
                        invert_sums(done)
                    if prev.valid and j in (1, 2):
                        newton_update(last_cols).then_inc(rn_ready, 1)
                    if done.valid and j != 3:
                        divide_o(done)
                    if mid.valid and j != 3:
                        row_max(mid, 1)
                    if cur.valid:
                        rotate(cur)
                    if after.valid:
                        add_residual(after)
                    if j == 0 and number and G == LAST:
                        cols = slice(2 * HEADS, 2 * HEADS + GT)
                        variances(y)
                        newton_seed(cols)
                        cubic_round(cols)
                        steps.mark(newton_round(cols))
                        dve.wait_ge(stored, FIRST_LAYER + 16 * (LAST - 2 - GROUPS))
                        normalise_tiles(y_out, y).then_inc(y_normed, 1)
                    if mid.valid and j != 1:
                        save_probs(mid)
                    if ffn:
                        dve.wait_ge(rn_ready, min(cur.t, DEPTH * TILES) if number else cur.t)
                        normalise_tiles(h2, h2).then_inc(h2_ready, 1)
                    if cur.valid:
                        sum_squares(cur)
                    if norm:
                        dve.wait_ge(h2_in, 64 * G)
                        variances(h2)
                    if final:
                        variances(y)
                    if cur.valid or norm or final:
                        cols = slice(0 if cur.valid else 2 * HEADS, 2 * HEADS + (GT if norm or final else 0))
                        if cur.valid:
                            need(dve, rot_scaled, cur.t)
                        else:
                            dve.wait_ge(rot_scaled, DEPTH * TILES)
                        newton_seed(cols)
                        cubic_round(cols)
                        if cur.valid and j in (0, 1):
                            newton_square(cols)
                            last_cols = cols
                        elif cur.valid:
                            newton_round(cols).then_inc(rn_ready, 1)
                        else:
                            steps.mark(newton_round(cols))
                    if final:
                        if cur.valid:
                            dve.wait_ge(rn_ready, cur.t + 1)
                        need(dve, stored, FIRST_LAYER + 16 * (G - 1 - GROUPS))
                        normalise_tiles(y_out, y).then_inc(y_normed, 1)
                    if j == 0 and not (number and not 0 <= G < LAST - 1):
                        split_inputs(G + 1)
                    if ffn:
                        split_h2(G - 1)
                    if j == 2:
                        if mid.valid:
                            invert_sums(mid)
                            divide_o(mid)
                        for half in range(2):
                            if prev.valid:
                                row_max(prev, half)
                    if ffn:
                        l = (G - 1) // GROUPS if number else layer
                        for c, (c0, cn) in enumerate(CHUNKS):
                            gate(G - 1, l, c, cn)
                        finish_group(G - 1, l)
                    elif j == 2 and number and G == 0:
                        dve.nop().then_inc(y_read, 1)
                        place_early(0)

            passes(dve, body, steps)


def kernel(L0_attn_x, L0_attn_W_hg, L0_attn_W_out, L0_ffn_wqkv, L0_ffn_q_scale, L0_ffn_k_scale, L0_ffn_wo,
           L0_ffn_ln_g, L0_ffn_ln_b, L0_ffn_w1, L0_ffn_b1, L0_ffn_w2, L0_ffn_b2):
    import concourse.bacc as bacc
    from concourse.bass_utils import run_bass_kernel_spmd

    tables = np.tile(rotary_tables().reshape(GROUPS, GT, P, TABW).transpose(0, 2, 1, 3), (DEPTH, 1, 1, 1))
    q_s, k_s = np.asarray(L0_ffn_q_scale), np.asarray(L0_ffn_k_scale)
    head_scales = np.repeat(np.concatenate([q_s, q_s, k_s, k_s], axis=1), GROUPS, axis=0)
    arrays = {
        "x": np.asarray(L0_attn_x).reshape(N, DIM),
        "w_hg_t": np.asarray(L0_attn_W_hg).T,
        "w_out_t": np.asarray(L0_attn_W_out).T,
        "wqkv": L0_ffn_wqkv, "wo": L0_ffn_wo,
        "ln_g": L0_ffn_ln_g, "ln_b": L0_ffn_ln_b, "w1": L0_ffn_w1, "b1": L0_ffn_b1, "w2": L0_ffn_w2,
        "b2": L0_ffn_b2, "tables": tables, "head_scales": head_scales, "consts": constant_block(),
    }
    arrays = {k: np.ascontiguousarray(v) for k, v in arrays.items()}
    nc = bacc.Bacc("TRN2", target_bir_lowering=False, num_devices=1)
    args = [nc.dram_tensor(k, a.shape, mybir.dt.from_np(a.dtype), kind="ExternalInput").ap() for k, a in arrays.items()]
    out = nc.dram_tensor("out", (N, DIM), F32, kind="ExternalOutput").ap()
    sandwich_kernel(nc, *args, out)
    r = run_bass_kernel_spmd(nc, [arrays], core_ids=[0])
    return r.results[0]["out"].reshape(1, N, DIM)
```
